# Optimizing a Trainium2 kernel written in Bass

```python
import numpy as np
import jax
import jax.numpy as jnp

def _softmax(x, axis=-1):
    return jax.nn.softmax(x, axis=axis)

def _gelu(x):
    return jax.nn.gelu(x, approximate=True)

def _silu(x):
    return jax.nn.silu(x)

def _sigmoid(x):
    return jax.nn.sigmoid(x)

def _layernorm(x, axis=-1, eps=1e-05):
    m = jnp.mean(x, axis=axis, keepdims=True)
    v = jnp.var(x, axis=axis, keepdims=True)
    return (x - m) / jnp.sqrt(v + eps)

def _scatter_add(tgt, idx, src, axis=0):
    return tgt.at[idx].add(src)

def _segment_sum(src, seg, n):
    return jax.ops.segment_sum(src, seg, n)
kernel_name = 'mk_decoder_preln_d4_seqx_r8_1f1ff6'

def setup_inputs(seed: int=0):
    np.random.seed(seed)
    _w = jnp.asarray

    def _rec_inputs():
        import jax
        import jax.numpy as jnp
        _rk = jax.random.key(seed)
        x = -0.0002928 + 1 * jax.random.normal(jax.random.fold_in(_rk, 1), (8, 256, 128), jnp.float32)
        _lenS = 256 - jax.random.randint(jax.random.fold_in(_rk, 7), (8,), 0, max(1, 256 // 4) + 1, jnp.int32)
        _lenS2 = 512 - jax.random.randint(jax.random.fold_in(_rk, 8), (8,), 0, max(1, 512 // 4) + 1, jnp.int32)
        _ctx_1024P = jax.random.normal(jax.random.fold_in(_rk, 11), (8, 16, 128), jnp.float32)
        _ctx_1024c = jax.random.dirichlet(jax.random.fold_in(_rk, 511), 0.3 * jnp.ones((16,), jnp.float32), (8, 512))
        _ctx_1024t = jnp.einsum('bsk,bkd->bsd', _ctx_1024c, _ctx_1024P)
        _ctx_1024t = _ctx_1024t * jax.lax.rsqrt(jnp.mean(jnp.square(_ctx_1024t)) + 1e-12) * 0.953939
        ctx_1024 = 2.81802e-05 + 1.00001 * (_ctx_1024t + 0.3 * jax.random.normal(jax.random.fold_in(_rk, 611), (8, 512, 128), jnp.float32))
        _validS = jnp.arange(256)[None, :] < _lenS[:, None]
        _validS2 = jnp.arange(512)[None, :] < _lenS2[:, None]
        _causal = jnp.tril(jnp.ones((256, 256), dtype=bool))
        mask_BxSxS2_ik1 = jnp.where(jnp.broadcast_to(_validS2[:, None, :], (8, 256, 512)), 1, 0).astype(jnp.int32)
        mask_SxS2_ik0 = jnp.where(jnp.broadcast_to(_validS2[0:1, :], (256, 512)), 0, 1).astype(jnp.int32)
        return (x, ctx_1024, mask_BxSxS2_ik1, mask_SxS2_ik0)
    x, ctx_1024, mask_BxSxS2_ik1, mask_SxS2_ik0 = _rec_inputs()

    def _L0_attn_setup():
        import jax, jax.numpy as jnp
        import numpy as np
        D_MODEL, N_HEADS, N_KV, HEAD_DIM, D_LAT = (128, 8, 2, 128, 32)
        N_REP = N_HEADS // N_KV
        B, T = (2, 256)
        key = jax.random.key(seed)
        ks = jax.random.split(key, 8)
        s = lambda fan_in: 1.0 / np.sqrt(fan_in)
        return {'x': jax.random.normal(ks[0], (B, T, D_MODEL), jnp.float32), 'wq': jax.random.normal(ks[1], (D_MODEL, N_HEADS * HEAD_DIM), jnp.float32) * s(D_MODEL), 'wk_down': jax.random.normal(ks[2], (D_MODEL, N_KV * D_LAT), jnp.float32) * s(D_MODEL), 'wv_down': jax.random.normal(ks[3], (D_MODEL, N_KV * D_LAT), jnp.float32) * s(D_MODEL), 'wk_up': jax.random.normal(ks[4], (D_LAT, HEAD_DIM), jnp.float32) * s(D_LAT), 'wv_up': jax.random.normal(ks[5], (D_LAT, HEAD_DIM), jnp.float32) * s(D_LAT), 'wo': jax.random.normal(ks[6], (N_HEADS * HEAD_DIM, D_MODEL), jnp.float32) * s(N_HEADS * HEAD_DIM)}
    _L0_attn_all = _L0_attn_setup()
    _L0_attn_in = {k: v for k, v in _L0_attn_all.items() if k in ('wq', 'wk_down', 'wv_down', 'wk_up', 'wv_up', 'wo')}
    del _L0_attn_all

    def _L0_xattn_setup():
        import jax, jax.numpy as jnp
        import numpy as np
        D_MODEL = 128
        N_HEADS = 16
        HEAD_DIM = D_MODEL // N_HEADS
        key = jax.random.key(seed)
        k1, k2, k3, k4, k5, k6 = jax.random.split(key, 6)
        B, T_q, T_kv = (4, 128, 512)
        s = 1.0 / np.sqrt(D_MODEL)
        return {'query': jax.random.normal(k1, (B, T_q, D_MODEL), dtype=jnp.float32), 'kv_source': jax.random.normal(k2, (B, T_kv, D_MODEL), dtype=jnp.float32), 'w_q': jax.random.normal(k3, (D_MODEL, D_MODEL), dtype=jnp.float32) * s, 'w_k': jax.random.normal(k4, (D_MODEL, D_MODEL), dtype=jnp.float32) * s, 'w_v': jax.random.normal(k5, (D_MODEL, D_MODEL), dtype=jnp.float32) * s, 'w_o': jax.random.normal(k6, (D_MODEL, D_MODEL), dtype=jnp.float32) * s}
    _L0_xattn_all = _L0_xattn_setup()
    _L0_xattn_in = {k: v for k, v in _L0_xattn_all.items() if k in ('w_q', 'w_k', 'w_v', 'w_o')}
    del _L0_xattn_all

    def _L0_ffn_setup():
        import jax, jax.numpy as jnp
        import numpy as np
        CAPACITY_FACTOR = 1.25
        key = jax.random.key(seed)
        k1, k2, k3, k4 = jax.random.split(key, 4)
        B, S, D, E, H = (2, 256, 128, 16, 512)
        inputs = jax.random.normal(k1, (B, S, D), dtype=jnp.float32)
        gate_w = jax.random.normal(k2, (E, D), dtype=jnp.float32) / np.float32(np.sqrt(D))
        w1 = jax.random.normal(k3, (E, D, H), dtype=jnp.float32) / np.float32(np.sqrt(D))
        w2 = jax.random.normal(k4, (E, H, D), dtype=jnp.float32) / np.float32(np.sqrt(H))
        return {'inputs': inputs, 'gate_w': gate_w, 'w1': w1, 'w2': w2}
    _L0_ffn_all = _L0_ffn_setup()
    _L0_ffn_in = {k: v for k, v in _L0_ffn_all.items() if k in ('gate_w', 'w1', 'w2')}
    del _L0_ffn_all

    def _L1_attn_setup():
        import jax, jax.numpy as jnp
        import numpy as np
        B, S, HID = (4, 128, 128)
        H = 8
        HD = HID // H
        NQ = 8
        RATIO = 0.5
        FF = 4 * HID
        EPS_COS = 1e-08
        LN_EPS = 1e-05

        def _layernorm(x, g, b):
            m = jnp.mean(x, axis=-1, keepdims=True)
            v = jnp.var(x, axis=-1, keepdims=True)
            return (x - m) * jax.lax.rsqrt(v + LN_EPS) * g + b
        key = jax.random.key(seed)
        ks = jax.random.split(key, 24)
        sc = 0.02
        inp = {'x': jax.random.normal(ks[0], (B, S, HID), jnp.float32), 'Wq': jax.random.normal(ks[1], (H, HID, HD)) * sc, 'bq': jnp.zeros((H, HD)), 'Wk': jax.random.normal(ks[2], (H, HID, HD)) * sc, 'bk': jnp.zeros((H, HD)), 'Wv': jax.random.normal(ks[3], (H, HID, HD)) * sc, 'bv': jnp.zeros((H, HD)), 'Wc2q': jax.random.normal(ks[4], (H, HD, NQ)) * sc, 'bc2q': jnp.zeros((H, NQ)), 'Wo': jax.random.normal(ks[5], (HID, HID)) * sc, 'bo': jnp.zeros((HID,)), 'g1': jnp.ones((HID,)), 'beta1': jnp.zeros((HID,)), 'g2': jnp.ones((HID,)), 'beta2': jnp.zeros((HID,)), 'W1': jax.random.normal(ks[6], (HID, FF)) * sc, 'b1': jnp.zeros((FF,)), 'Wm': jax.random.normal(ks[7], (FF, NQ)) * sc, 'bm': jnp.zeros((NQ,)), 'Wqo': jax.random.normal(ks[8], (NQ, FF)) * sc, 'bqo': jnp.zeros((FF,)), 'W2': jax.random.normal(ks[9], (FF, HID)) * sc, 'b2': jnp.zeros((HID,))}
        return inp
    _L1_attn_all = _L1_attn_setup()
    _L1_attn_in = {k: v for k, v in _L1_attn_all.items() if k in ('Wq', 'bq', 'Wk', 'bk', 'Wv', 'bv', 'Wc2q', 'bc2q', 'Wo', 'bo', 'g1', 'beta1', 'g2', 'beta2', 'W1', 'b1', 'Wm', 'bm', 'Wqo', 'bqo', 'W2', 'b2')}
    del _L1_attn_all

    def _L1_xattn_setup():
        import jax, jax.numpy as jnp
        import numpy as np
        HIDDEN = 128
        NUM_HEADS = 16
        HEAD_DIM = HIDDEN // NUM_HEADS
        SCALE = 1.0 / float(np.sqrt(HEAD_DIM))
        key = jax.random.key(seed)
        ks = jax.random.split(key, 10)
        B, SQ, SKV = (2, 256, 512)
        init = 0.02
        return {'query_states': jax.random.normal(ks[0], (B, SQ, HIDDEN), dtype=jnp.float32), 'key_value_states': jax.random.normal(ks[1], (B, SKV, HIDDEN), dtype=jnp.float32), 'Wq': jax.random.normal(ks[2], (HIDDEN, HIDDEN), dtype=jnp.float32) * init, 'bq': jnp.zeros((HIDDEN,), dtype=jnp.float32), 'Wk': jax.random.normal(ks[3], (HIDDEN, HIDDEN), dtype=jnp.float32) * init, 'bk': jnp.zeros((HIDDEN,), dtype=jnp.float32), 'Wv': jax.random.normal(ks[4], (HIDDEN, HIDDEN), dtype=jnp.float32) * init, 'bv': jnp.zeros((HIDDEN,), dtype=jnp.float32), 'Wo': jax.random.normal(ks[5], (HIDDEN, HIDDEN), dtype=jnp.float32) * init, 'bo': jnp.zeros((HIDDEN,), dtype=jnp.float32)}
    _L1_xattn_all = _L1_xattn_setup()
    _L1_xattn_in = {k: v for k, v in _L1_xattn_all.items() if k in ('Wq', 'bq', 'Wk', 'bk', 'Wv', 'bv', 'Wo', 'bo')}
    del _L1_xattn_all

    def _L1_ffn_setup():
        import jax, jax.numpy as jnp
        import numpy as np
        B, N, D, E, DFF = (4, 256, 128, 16, 512)
        CAPACITY_FACTOR = 2.0
        CAP = int(N * CAPACITY_FACTOR / E)
        SINKHORN_ITERS = 6

        def _sinkhorn(logits, n_iters=SINKHORN_ITERS, tau=1.0):
            t = logits / tau
            for _ in range(n_iters):
                t = t - jax.scipy.special.logsumexp(t, axis=-2, keepdims=True)
                t = t - jax.scipy.special.logsumexp(t, axis=-1, keepdims=True)
            return jnp.exp(t)
        key = jax.random.key(seed)
        ks = jax.random.split(key, 6)
        scaled = lambda k, sh, fan: (jax.random.normal(k, sh, jnp.float32) / np.sqrt(fan)).astype(jnp.float32)
        return {'x': jax.random.normal(ks[0], (B, N, D), jnp.float32), 'gate_query': scaled(ks[1], (E, D), D), 'log_temp': jnp.asarray(np.log(0.5), jnp.float32), 'w1': scaled(ks[2], (E, D, DFF), D), 'b1': jnp.zeros((E, DFF), jnp.float32), 'w2': scaled(ks[3], (E, DFF, D), DFF), 'b2': jnp.zeros((E, D), jnp.float32)}
    _L1_ffn_all = _L1_ffn_setup()
    _L1_ffn_in = {k: v for k, v in _L1_ffn_all.items() if k in ('gate_query', 'log_temp', 'w1', 'b1', 'w2', 'b2')}
    del _L1_ffn_all

    def _L2_attn_setup():
        import jax, jax.numpy as jnp
        import numpy as np
        HEADS = 16
        KV_HEADS = 4
        DIM_HEAD = 64
        SCALE = DIM_HEAD ** (-0.5)

        def _rotate_half(x):
            x1, x2 = jnp.split(x, 2, axis=-1)
            return jnp.concatenate((-x2, x1), axis=-1)

        def _rope_freqs(n, d):
            inv_freq = 1.0 / 10000.0 ** (jnp.arange(0, d, 2, dtype=jnp.float32) / d)
            freqs = jnp.einsum('i,j->ij', jnp.arange(n, dtype=jnp.float32), inv_freq)
            return jnp.concatenate((freqs, freqs), axis=-1)
        key = jax.random.key(seed)
        ks = jax.random.split(key, 4)
        b, n, dim = (2, 256, 128)
        inner = HEADS * DIM_HEAD
        s = dim ** (-0.5)
        return {'x': jax.random.normal(ks[0], (b, n, dim), jnp.float32), 'Wq': jax.random.normal(ks[1], (dim, inner), jnp.float32) * s, 'Wkv': jax.random.normal(ks[2], (dim, DIM_HEAD * KV_HEADS * 2), jnp.float32) * s, 'Wo': jax.random.normal(ks[3], (inner, dim), jnp.float32) * s, 'bo': jnp.zeros((dim,), jnp.float32)}
    _L2_attn_all = _L2_attn_setup()
    _L2_attn_in = {k: v for k, v in _L2_attn_all.items() if k in ('Wq', 'Wkv', 'Wo', 'bo')}
    del _L2_attn_all

    def _L2_xattn_setup():
        import jax, jax.numpy as jnp
        import numpy as np
        D_MODEL, D_K, D_V = (128, 128, 128)
        B, S = (8, 256)
        key = jax.random.key(seed)
        ks = jax.random.split(key, 10)
        s = 1.0 / np.sqrt(D_MODEL)
        return {'Q': jax.random.normal(ks[0], (B, S, D_MODEL), jnp.float32), 'K': jax.random.normal(ks[1], (B, S, D_MODEL), jnp.float32), 'V': jax.random.normal(ks[2], (B, S, D_MODEL), jnp.float32), 'mask': jax.random.randint(ks[3], (B, S, S), 0, 2, jnp.int32), 'Wq': jax.random.uniform(ks[4], (D_MODEL, D_K), jnp.float32, -s, s), 'bq': jnp.zeros((D_K,), jnp.float32), 'Wk': jax.random.uniform(ks[5], (D_MODEL, D_K), jnp.float32, -s, s), 'bk': jnp.zeros((D_K,), jnp.float32), 'Wv': jax.random.uniform(ks[6], (D_MODEL, D_V), jnp.float32, -s, s), 'bv': jnp.zeros((D_V,), jnp.float32)}
    _L2_xattn_all = _L2_xattn_setup()
    _L2_xattn_in = {k: v for k, v in _L2_xattn_all.items() if k in ('Wq', 'bq', 'Wk', 'bk', 'Wv', 'bv')}
    del _L2_xattn_all

    def _L2_ffn_setup():
        import jax, jax.numpy as jnp
        import numpy as np
        TOP_K = 2

        def _ffn(x, gw, uw, dw):
            return jax.nn.silu(x @ gw.T) * (x @ uw.T) @ dw.T
        key = jax.random.key(seed)
        ks = jax.random.split(key, 8)
        w = lambda k, shape: jax.random.normal(k, shape, jnp.float32) * 0.02
        return dict(x=jax.random.normal(ks[0], (4, 256, 128), jnp.float32), gate_w=w(ks[1], (8, 128)), expert_gate=w(ks[2], (8, 352, 128)), expert_up=w(ks[3], (8, 352, 128)), expert_down=w(ks[4], (8, 128, 352)), shared_gate=w(ks[5], (352, 128)), shared_up=w(ks[6], (352, 128)), shared_down=w(ks[7], (128, 352)))
    _L2_ffn_all = _L2_ffn_setup()
    _L2_ffn_in = {k: v for k, v in _L2_ffn_all.items() if k in ('gate_w', 'expert_gate', 'expert_up', 'expert_down', 'shared_gate', 'shared_up', 'shared_down')}
    del _L2_ffn_all

    def _L3_attn_setup():
        import jax, jax.numpy as jnp
        import numpy as np
        NUM_HEADS = 16
        HEAD_DIM = 64
        key = jax.random.key(seed)
        k1, k2, k3, k4 = jax.random.split(key, 4)
        B, L, E = (2, 256, 128)
        H, D = (NUM_HEADS, HEAD_DIM)
        scale = 0.02
        x = jax.random.normal(k1, (B, L, E), dtype=jnp.float32)
        Wa = jax.random.normal(k2, (3 * H * D, E), dtype=jnp.float32) * scale
        Wout_w = jax.random.normal(k3, (E, H * D), dtype=jnp.float32) * scale
        Wout_b = jax.random.normal(k4, (E,), dtype=jnp.float32) * scale
        return {'x': x, 'Wa': Wa, 'Wout_w': Wout_w, 'Wout_b': Wout_b}
    _L3_attn_all = _L3_attn_setup()
    _L3_attn_in = {k: v for k, v in _L3_attn_all.items() if k in ('Wa', 'Wout_w', 'Wout_b')}
    del _L3_attn_all

    def _L3_xattn_setup():
        import jax, jax.numpy as jnp
        import numpy as np
        D_MODEL = 128
        NUM_HEADS = 16
        D_K = D_MODEL // NUM_HEADS
        BATCH = 4
        SEQ = 256

        def _split_heads(x):
            b, s, _ = x.shape
            return x.reshape(b, s, NUM_HEADS, D_K).transpose(0, 2, 1, 3)
        key = jax.random.key(seed)
        ks = jax.random.split(key, 12)
        s = 0.02
        inp = {'Q': jax.random.normal(ks[0], (BATCH, SEQ, D_MODEL), jnp.float32), 'K': jax.random.normal(ks[1], (BATCH, SEQ, D_MODEL), jnp.float32), 'V': jax.random.normal(ks[2], (BATCH, SEQ, D_MODEL), jnp.float32), 'mask': jnp.tril(jnp.ones((SEQ, SEQ), jnp.int32)), 'Wq': jax.random.normal(ks[3], (D_MODEL, D_MODEL), jnp.float32) * s, 'bq': jax.random.normal(ks[4], (D_MODEL,), jnp.float32) * s, 'Wk': jax.random.normal(ks[5], (D_MODEL, D_MODEL), jnp.float32) * s, 'bk': jax.random.normal(ks[6], (D_MODEL,), jnp.float32) * s, 'Wv': jax.random.normal(ks[7], (D_MODEL, D_MODEL), jnp.float32) * s, 'bv': jax.random.normal(ks[8], (D_MODEL,), jnp.float32) * s, 'Wo': jax.random.normal(ks[9], (D_MODEL, D_MODEL), jnp.float32) * s, 'bo': jax.random.normal(ks[10], (D_MODEL,), jnp.float32) * s}
        return inp
    _L3_xattn_all = _L3_xattn_setup()
    _L3_xattn_in = {k: v for k, v in _L3_xattn_all.items() if k in ('Wq', 'bq', 'Wk', 'bk', 'Wv', 'bv', 'Wo', 'bo')}
    del _L3_xattn_all

    def _L3_ffn_setup():
        import jax, jax.numpy as jnp
        import numpy as np
        B, K, D = (128, 32, 128)
        E = 32
        H = int(D * 0.25)

        def _rsqrt_uniform(key, shape, d):
            bound = d ** (-0.5)
            return jax.random.uniform(key, shape, jnp.float32, -bound, bound)
        key = jax.random.key(seed)
        ks = jax.random.split(key, 7)
        return {'x': jax.random.normal(ks[0], (B, K, D), jnp.float32), 'router_w': _rsqrt_uniform(ks[1], (E, D), D), 'router_b': _rsqrt_uniform(ks[2], (E,), D), 'weights1': _rsqrt_uniform(ks[3], (E, D, H), H), 'bias1': _rsqrt_uniform(ks[4], (E, H), H), 'weights2': _rsqrt_uniform(ks[5], (E, H, D), D), 'bias2': _rsqrt_uniform(ks[6], (E, D), D)}
    _L3_ffn_all = _L3_ffn_setup()
    _L3_ffn_in = {k: v for k, v in _L3_ffn_all.items() if k in ('router_w', 'router_b', 'weights1', 'bias1', 'weights2', 'bias2')}
    del _L3_ffn_all
    return {'x': x, 'ctx_1024': ctx_1024, 'mask_BxSxS2_ik1': mask_BxSxS2_ik1, 'mask_SxS2_ik0': mask_SxS2_ik0, 'L0_attn_wq': _L0_attn_in['wq'], 'L0_attn_wk_down': _L0_attn_in['wk_down'], 'L0_attn_wv_down': _L0_attn_in['wv_down'], 'L0_attn_wk_up': _L0_attn_in['wk_up'], 'L0_attn_wv_up': _L0_attn_in['wv_up'], 'L0_attn_wo': _L0_attn_in['wo'], 'L0_xattn_w_q': _L0_xattn_in['w_q'], 'L0_xattn_w_k': _L0_xattn_in['w_k'], 'L0_xattn_w_v': _L0_xattn_in['w_v'], 'L0_xattn_w_o': _L0_xattn_in['w_o'], 'L0_ffn_gate_w': _L0_ffn_in['gate_w'], 'L0_ffn_w1': _L0_ffn_in['w1'], 'L0_ffn_w2': _L0_ffn_in['w2'], 'L1_attn_Wq': _L1_attn_in['Wq'], 'L1_attn_bq': _L1_attn_in['bq'], 'L1_attn_Wk': _L1_attn_in['Wk'], 'L1_attn_bk': _L1_attn_in['bk'], 'L1_attn_Wv': _L1_attn_in['Wv'], 'L1_attn_bv': _L1_attn_in['bv'], 'L1_attn_Wc2q': _L1_attn_in['Wc2q'], 'L1_attn_bc2q': _L1_attn_in['bc2q'], 'L1_attn_Wo': _L1_attn_in['Wo'], 'L1_attn_bo': _L1_attn_in['bo'], 'L1_attn_g1': _L1_attn_in['g1'], 'L1_attn_beta1': _L1_attn_in['beta1'], 'L1_attn_g2': _L1_attn_in['g2'], 'L1_attn_beta2': _L1_attn_in['beta2'], 'L1_attn_W1': _L1_attn_in['W1'], 'L1_attn_b1': _L1_attn_in['b1'], 'L1_attn_Wm': _L1_attn_in['Wm'], 'L1_attn_bm': _L1_attn_in['bm'], 'L1_attn_Wqo': _L1_attn_in['Wqo'], 'L1_attn_bqo': _L1_attn_in['bqo'], 'L1_attn_W2': _L1_attn_in['W2'], 'L1_attn_b2': _L1_attn_in['b2'], 'L1_xattn_Wq': _L1_xattn_in['Wq'], 'L1_xattn_bq': _L1_xattn_in['bq'], 'L1_xattn_Wk': _L1_xattn_in['Wk'], 'L1_xattn_bk': _L1_xattn_in['bk'], 'L1_xattn_Wv': _L1_xattn_in['Wv'], 'L1_xattn_bv': _L1_xattn_in['bv'], 'L1_xattn_Wo': _L1_xattn_in['Wo'], 'L1_xattn_bo': _L1_xattn_in['bo'], 'L1_ffn_gate_query': _L1_ffn_in['gate_query'], 'L1_ffn_log_temp': _L1_ffn_in['log_temp'], 'L1_ffn_w1': _L1_ffn_in['w1'], 'L1_ffn_b1': _L1_ffn_in['b1'], 'L1_ffn_w2': _L1_ffn_in['w2'], 'L1_ffn_b2': _L1_ffn_in['b2'], 'L2_attn_Wq': _L2_attn_in['Wq'], 'L2_attn_Wkv': _L2_attn_in['Wkv'], 'L2_attn_Wo': _L2_attn_in['Wo'], 'L2_attn_bo': _L2_attn_in['bo'], 'L2_xattn_Wq': _L2_xattn_in['Wq'], 'L2_xattn_bq': _L2_xattn_in['bq'], 'L2_xattn_Wk': _L2_xattn_in['Wk'], 'L2_xattn_bk': _L2_xattn_in['bk'], 'L2_xattn_Wv': _L2_xattn_in['Wv'], 'L2_xattn_bv': _L2_xattn_in['bv'], 'L2_ffn_gate_w': _L2_ffn_in['gate_w'], 'L2_ffn_expert_gate': _L2_ffn_in['expert_gate'], 'L2_ffn_expert_up': _L2_ffn_in['expert_up'], 'L2_ffn_expert_down': _L2_ffn_in['expert_down'], 'L2_ffn_shared_gate': _L2_ffn_in['shared_gate'], 'L2_ffn_shared_up': _L2_ffn_in['shared_up'], 'L2_ffn_shared_down': _L2_ffn_in['shared_down'], 'L3_attn_Wa': _L3_attn_in['Wa'], 'L3_attn_Wout_w': _L3_attn_in['Wout_w'], 'L3_attn_Wout_b': _L3_attn_in['Wout_b'], 'L3_xattn_Wq': _L3_xattn_in['Wq'], 'L3_xattn_bq': _L3_xattn_in['bq'], 'L3_xattn_Wk': _L3_xattn_in['Wk'], 'L3_xattn_bk': _L3_xattn_in['bk'], 'L3_xattn_Wv': _L3_xattn_in['Wv'], 'L3_xattn_bv': _L3_xattn_in['bv'], 'L3_xattn_Wo': _L3_xattn_in['Wo'], 'L3_xattn_bo': _L3_xattn_in['bo'], 'L3_ffn_router_w': _L3_ffn_in['router_w'], 'L3_ffn_router_b': _L3_ffn_in['router_b'], 'L3_ffn_weights1': _L3_ffn_in['weights1'], 'L3_ffn_bias1': _L3_ffn_in['bias1'], 'L3_ffn_weights2': _L3_ffn_in['weights2'], 'L3_ffn_bias2': _L3_ffn_in['bias2']}

def reference(x, ctx_1024, mask_BxSxS2_ik1, mask_SxS2_ik0, L0_attn_wq, L0_attn_wk_down, L0_attn_wv_down, L0_attn_wk_up, L0_attn_wv_up, L0_attn_wo, L0_xattn_w_q, L0_xattn_w_k, L0_xattn_w_v, L0_xattn_w_o, L0_ffn_gate_w, L0_ffn_w1, L0_ffn_w2, L1_attn_Wq, L1_attn_bq, L1_attn_Wk, L1_attn_bk, L1_attn_Wv, L1_attn_bv, L1_attn_Wc2q, L1_attn_bc2q, L1_attn_Wo, L1_attn_bo, L1_attn_g1, L1_attn_beta1, L1_attn_g2, L1_attn_beta2, L1_attn_W1, L1_attn_b1, L1_attn_Wm, L1_attn_bm, L1_attn_Wqo, L1_attn_bqo, L1_attn_W2, L1_attn_b2, L1_xattn_Wq, L1_xattn_bq, L1_xattn_Wk, L1_xattn_bk, L1_xattn_Wv, L1_xattn_bv, L1_xattn_Wo, L1_xattn_bo, L1_ffn_gate_query, L1_ffn_log_temp, L1_ffn_w1, L1_ffn_b1, L1_ffn_w2, L1_ffn_b2, L2_attn_Wq, L2_attn_Wkv, L2_attn_Wo, L2_attn_bo, L2_xattn_Wq, L2_xattn_bq, L2_xattn_Wk, L2_xattn_bk, L2_xattn_Wv, L2_xattn_bv, L2_ffn_gate_w, L2_ffn_expert_gate, L2_ffn_expert_up, L2_ffn_expert_down, L2_ffn_shared_gate, L2_ffn_shared_up, L2_ffn_shared_down, L3_attn_Wa, L3_attn_Wout_w, L3_attn_Wout_b, L3_xattn_Wq, L3_xattn_bq, L3_xattn_Wk, L3_xattn_bk, L3_xattn_Wv, L3_xattn_bv, L3_xattn_Wo, L3_xattn_bo, L3_ffn_router_w, L3_ffn_router_b, L3_ffn_weights1, L3_ffn_bias1, L3_ffn_weights2, L3_ffn_bias2):
    import jax
    import jax.numpy as jnp

    def _L0_attn_ref(x, wq, wk_down, wv_down, wk_up, wv_up, wo):
        import jax, jax.numpy as jnp
        import numpy as np
        D_MODEL, N_HEADS, N_KV, HEAD_DIM, D_LAT = (128, 8, 2, 128, 32)
        N_REP = N_HEADS // N_KV
        B, T = (2, 256)
        Bq, Tq, _ = x.shape
        scale = HEAD_DIM ** (-0.5)
        q = (x @ wq).reshape(Bq, Tq, N_KV, N_REP, HEAD_DIM)
        k_lat = (x @ wk_down).reshape(Bq, Tq, N_KV, D_LAT)
        v_lat = (x @ wv_down).reshape(Bq, Tq, N_KV, D_LAT)
        k = jnp.einsum('bkhl,ld->bkhd', k_lat, wk_up)
        v = jnp.einsum('bkhl,ld->bkhd', v_lat, wv_up)
        scores = jnp.einsum('bqhrd,bkhd->bhrqk', q, k) * scale
        causal = jnp.tril(jnp.ones((Tq, Tq), dtype=bool))
        scores = jnp.where(causal, scores, jnp.finfo(scores.dtype).min)
        probs = jax.nn.softmax(scores, axis=-1)
        y = jnp.einsum('bhrqk,bkhd->bqhrd', probs, v)
        y = y.reshape(Bq, Tq, N_HEADS * HEAD_DIM)
        return y @ wo

    def _L0_xattn_ref(query, kv_source, w_q, w_k, w_v, w_o):
        import jax, jax.numpy as jnp
        import numpy as np
        D_MODEL = 128
        N_HEADS = 16
        HEAD_DIM = D_MODEL // N_HEADS
        B, T_q, _ = query.shape
        T_kv = kv_source.shape[1]
        q = (query @ w_q.T).reshape(B, T_q, N_HEADS, HEAD_DIM)
        k = (kv_source @ w_k.T).reshape(B, T_kv, N_HEADS, HEAD_DIM)
        v = (kv_source @ w_v.T).reshape(B, T_kv, N_HEADS, HEAD_DIM)
        scale = HEAD_DIM ** (-0.5)
        attn = jax.nn.softmax(jnp.einsum('bqhd,bkhd->bhqk', q, k) * scale, axis=-1)
        out = jnp.einsum('bhqk,bkhd->bqhd', attn, v).reshape(B, T_q, D_MODEL)
        return out @ w_o.T

    def _L0_ffn_ref(inputs, gate_w, w1, w2):
        import jax, jax.numpy as jnp
        import numpy as np
        CAPACITY_FACTOR = 1.25
        orig_shape = inputs.shape
        D = orig_shape[-1]
        tokens = inputs.reshape(-1, D)
        T = tokens.shape[0]
        E = gate_w.shape[0]
        C = int(CAPACITY_FACTOR * T / E)
        logits = tokens @ gate_w.T
        probs = jax.nn.softmax(logits, axis=-1)
        expert_idx = jnp.argmax(probs, axis=-1)
        mask = jax.nn.one_hot(expert_idx, E, dtype=jnp.int32)
        locations = jnp.cumsum(mask, axis=0) - 1
        mask = mask * (locations < C)
        loc_oh = jax.nn.one_hot(locations, C, dtype=probs.dtype)
        sec_mask = mask[:, :, None].astype(probs.dtype) * loc_oh
        combine_weights = probs[:, :, None] * sec_mask
        dispatch = jnp.einsum('tec,td->ecd', sec_mask, tokens)
        h = jax.nn.relu(jnp.einsum('ecd,edh->ech', dispatch, w1))
        expert_out = jnp.einsum('ech,ehd->ecd', h, w2)
        ans = jnp.einsum('tec,ecd->td', combine_weights, expert_out)
        return ans.reshape(orig_shape)

    def _L1_attn_ref(x, Wq, bq, Wk, bk, Wv, bv, Wc2q, bc2q, Wo, bo, g1, beta1, g2, beta2, W1, b1, Wm, bm, Wqo, bqo, W2, b2):
        import jax, jax.numpy as jnp
        import numpy as np
        B, S, HID = (4, 128, 128)
        H = 8
        HD = HID // H
        NQ = 8
        RATIO = 0.5
        FF = 4 * HID
        EPS_COS = 1e-08
        LN_EPS = 1e-05

        def _layernorm(x, g, b):
            m = jnp.mean(x, axis=-1, keepdims=True)
            v = jnp.var(x, axis=-1, keepdims=True)
            return (x - m) * jax.lax.rsqrt(v + LN_EPS) * g + b
        Q = jnp.einsum('bsh,nhd->bnsd', x, Wq) + bq[None, :, None, :]
        K = jnp.einsum('bsh,nhd->bnsd', x, Wk) + bk[None, :, None, :]
        V = jnp.einsum('bsh,nhd->bnsd', x, Wv) + bv[None, :, None, :]
        qq = jnp.einsum('bnsd,ndq->bnsq', Q, Wc2q) + bc2q[None, :, None, :]
        kq = jnp.einsum('bnsd,ndq->bnsq', K, Wc2q) + bc2q[None, :, None, :]
        qn = jnp.linalg.norm(qq, axis=-1)
        kn = jnp.linalg.norm(kq, axis=-1)
        dots = jnp.einsum('bnsq,bntq->bnst', qq, kq)
        fid = dots / jnp.maximum(qn[..., :, None] * kn[..., None, :], EPS_COS)
        qw = fid * (1.0 + 0.1 * jnp.sin(fid * jnp.pi))
        cw = jnp.einsum('bnsd,bntd->bnst', Q, K) / np.sqrt(HD).astype(np.float32)
        aw = RATIO * qw + (1.0 - RATIO) * cw
        probs = jax.nn.softmax(aw, axis=-1)
        heads = jnp.einsum('bnst,bntd->bnsd', probs, V)
        attn = heads.transpose(0, 2, 1, 3).reshape(x.shape[0], x.shape[1], HID)
        attn = attn @ Wo + bo
        x1 = _layernorm(x + attn, g1, beta1)
        h = x1 @ W1 + b1
        qm = h @ Wm + bm
        qe = jnp.tanh(qm) * jnp.cos(qm * (jnp.pi / 4))
        ha = qe @ Wqo + bqo
        ff = ha @ W2 + b2
        out = _layernorm(x1 + ff, g2, beta2)
        return out

    def _L1_xattn_ref(query_states, key_value_states, Wq, bq, Wk, bk, Wv, bv, Wo, bo):
        import jax, jax.numpy as jnp
        import numpy as np
        HIDDEN = 128
        NUM_HEADS = 16
        HEAD_DIM = HIDDEN // NUM_HEADS
        SCALE = 1.0 / float(np.sqrt(HEAD_DIM))
        B, SQ, _ = query_states.shape
        _, SKV, _ = key_value_states.shape
        q = query_states @ Wq.T + bq
        k = key_value_states @ Wk.T + bk
        v = key_value_states @ Wv.T + bv
        q = q.reshape(B, SQ, NUM_HEADS, HEAD_DIM).transpose(0, 2, 1, 3) * SCALE
        k = k.reshape(B, SKV, NUM_HEADS, HEAD_DIM).transpose(0, 2, 1, 3)
        v = v.reshape(B, SKV, NUM_HEADS, HEAD_DIM).transpose(0, 2, 1, 3)
        scores = jnp.einsum('bhqd,bhkd->bhqk', q, k)
        attn = jax.nn.softmax(scores, axis=-1)
        ctx = jnp.einsum('bhqk,bhkd->bhqd', attn, v)
        ctx = ctx.transpose(0, 2, 1, 3).reshape(B, SQ, HIDDEN)
        return ctx @ Wo.T + bo

    def _L1_ffn_ref(x, gate_query, log_temp, w1, b1, w2, b2):
        import jax, jax.numpy as jnp
        import numpy as np
        B, N, D, E, DFF = (4, 256, 128, 16, 512)
        CAPACITY_FACTOR = 2.0
        CAP = int(N * CAPACITY_FACTOR / E)
        SINKHORN_ITERS = 6

        def _sinkhorn(logits, n_iters=SINKHORN_ITERS, tau=1.0):
            t = logits / tau
            for _ in range(n_iters):
                t = t - jax.scipy.special.logsumexp(t, axis=-2, keepdims=True)
                t = t - jax.scipy.special.logsumexp(t, axis=-1, keepdims=True)
            return jnp.exp(t)
        b, n, d = x.shape
        gate_logits = jnp.einsum('bnd,ed->ben', x, gate_query)
        affinity_logits = gate_logits / jnp.exp(log_temp)
        affinity = _sinkhorn(affinity_logits)
        gates, idx = jax.lax.top_k(affinity, CAP)
        expert_in = jnp.take_along_axis(x[:, None, :, :], idx[..., None], axis=2)
        h = jax.nn.gelu(jnp.einsum('becd,edf->becf', expert_in, w1) + b1[None, :, None, :])
        expert_out = jnp.einsum('becf,efd->becd', h, w2) + b2[None, :, None, :]
        out = jnp.zeros_like(x)
        out = out.at[jnp.arange(b)[:, None, None], idx].add(gates[..., None] * expert_out)
        return out

    def _L2_attn_ref(x, Wq, Wkv, Wo, bo):
        import jax, jax.numpy as jnp
        import numpy as np
        HEADS = 16
        KV_HEADS = 4
        DIM_HEAD = 64
        SCALE = DIM_HEAD ** (-0.5)

        def _rotate_half(x):
            x1, x2 = jnp.split(x, 2, axis=-1)
            return jnp.concatenate((-x2, x1), axis=-1)

        def _rope_freqs(n, d):
            inv_freq = 1.0 / 10000.0 ** (jnp.arange(0, d, 2, dtype=jnp.float32) / d)
            freqs = jnp.einsum('i,j->ij', jnp.arange(n, dtype=jnp.float32), inv_freq)
            return jnp.concatenate((freqs, freqs), axis=-1)
        b, n, dim = x.shape
        g = HEADS // KV_HEADS
        q = (x @ Wq).reshape(b, n, HEADS, DIM_HEAD).transpose(0, 2, 1, 3)
        kv = (x @ Wkv).reshape(b, n, 2 * KV_HEADS, DIM_HEAD)
        k = kv[:, :, :KV_HEADS].transpose(0, 2, 1, 3)
        v = kv[:, :, KV_HEADS:].transpose(0, 2, 1, 3)
        freqs = _rope_freqs(n, DIM_HEAD)
        cos, sin = (jnp.cos(freqs), jnp.sin(freqs))
        q = q * cos + _rotate_half(q) * sin
        k = k * cos + _rotate_half(k) * sin
        k = jnp.repeat(k, g, axis=1)
        v = jnp.repeat(v, g, axis=1)
        dots = jnp.einsum('bhid,bhjd->bhij', q, k) * SCALE
        attn = jax.nn.softmax(dots, axis=-1)
        out = jnp.einsum('bhij,bhjd->bhid', attn, v)
        out = out.transpose(0, 2, 1, 3).reshape(b, n, HEADS * DIM_HEAD)
        return out @ Wo + bo

    def _L2_xattn_ref(Q, K, V, mask, Wq, bq, Wk, bk, Wv, bv):
        import jax, jax.numpy as jnp
        import numpy as np
        D_MODEL, D_K, D_V = (128, 128, 128)
        B, S = (8, 256)
        pq = Q @ Wq + bq
        pk = K @ Wk + bk
        pv = V @ Wv + bv
        scores = jnp.einsum('bqd,bkd->bqk', pq, pk)
        masked = jnp.where(mask == 1, jnp.float32(-1000000000.0), scores)
        weights = jax.nn.softmax(masked / jnp.sqrt(jnp.float32(D_K)), axis=-1)
        return jnp.einsum('bqk,bkd->bqd', weights, pv)

    def _L2_ffn_ref(x, gate_w, expert_gate, expert_up, expert_down, shared_gate, shared_up, shared_down):
        import jax, jax.numpy as jnp
        import numpy as np
        TOP_K = 2

        def _ffn(x, gw, uw, dw):
            return jax.nn.silu(x @ gw.T) * (x @ uw.T) @ dw.T
        B, S, H = x.shape
        xf = x.reshape(-1, H)
        T = xf.shape[0]
        E = expert_gate.shape[0]
        shared = _ffn(xf, shared_gate, shared_up, shared_down)
        logits = xf @ gate_w.T
        probs = jax.nn.softmax(logits, axis=-1)
        topw, topi = jax.lax.top_k(probs, TOP_K)
        topw = topw / (topw.sum(-1, keepdims=True) + 1e-20)
        comb = jnp.zeros((T, E), xf.dtype).at[jnp.arange(T)[:, None], topi].add(topw)

        def body(acc, ws):
            gw, uw, dw, wcol = ws
            return (acc + _ffn(xf, gw, uw, dw) * wcol[:, None], None)
        routed, _ = jax.lax.scan(body, jnp.zeros_like(xf), (expert_gate, expert_up, expert_down, comb.T))
        return (shared + routed).reshape(B, S, H)

    def _L3_attn_ref(x, Wa, Wout_w, Wout_b):
        import jax, jax.numpy as jnp
        import numpy as np
        NUM_HEADS = 16
        HEAD_DIM = 64
        B, L, E = x.shape
        H, D = (NUM_HEADS, HEAD_DIM)
        tmp = jnp.einsum('ble,fe->blf', x, Wa)
        tmp = tmp.reshape(B, L, H, 3 * D).transpose(0, 2, 1, 3)
        q, k, v = jnp.split(tmp, 3, axis=3)
        A = jnp.einsum('bhqd,bhkd->bhqk', q, k) / np.sqrt(D).astype(np.float32)
        causal = jnp.tril(jnp.ones((L, L), dtype=bool))
        A = jnp.where(causal[None, None, :, :], A, -jnp.inf)
        A = jax.nn.softmax(A, axis=-1)
        o = jnp.einsum('bhqk,bhkd->bhqd', A, v)
        o = o.transpose(0, 2, 1, 3).reshape(B, L, H * D)
        out = jnp.einsum('blf,of->blo', o, Wout_w) + Wout_b
        return out

    def _L3_xattn_ref(Q, K, V, mask, Wq, bq, Wk, bk, Wv, bv, Wo, bo):
        import jax, jax.numpy as jnp
        import numpy as np
        D_MODEL = 128
        NUM_HEADS = 16
        D_K = D_MODEL // NUM_HEADS
        BATCH = 4
        SEQ = 256

        def _split_heads(x):
            b, s, _ = x.shape
            return x.reshape(b, s, NUM_HEADS, D_K).transpose(0, 2, 1, 3)
        q = _split_heads(Q @ Wq.T + bq)
        k = _split_heads(K @ Wk.T + bk)
        v = _split_heads(V @ Wv.T + bv)
        scale = 1.0 / jnp.sqrt(jnp.asarray(D_K, q.dtype))
        scores = jnp.einsum('bhqd,bhkd->bhqk', q, k) * scale
        scores = jnp.where(mask == 0, jnp.asarray(-jnp.inf, scores.dtype), scores)
        attn = jax.nn.softmax(scores, axis=-1)
        out = jnp.einsum('bhqk,bhkd->bhqd', attn, v)
        b, h, s, dk = out.shape
        out = out.transpose(0, 2, 1, 3).reshape(b, s, h * dk)
        return out @ Wo.T + bo

    def _L3_ffn_ref(x, router_w, router_b, weights1, bias1, weights2, bias2):
        import jax, jax.numpy as jnp
        import numpy as np
        B, K, D = (128, 32, 128)
        E = 32
        H = int(D * 0.25)

        def _rsqrt_uniform(key, shape, d):
            bound = d ** (-0.5)
            return jax.random.uniform(key, shape, jnp.float32, -bound, bound)
        b, k, d = x.shape
        x_flat = x.reshape(-1, d)
        n = x_flat.shape[0]
        logits = x_flat @ router_w.T + router_b
        routed_idx = jnp.argmax(logits, axis=-1)

        def expert_mlp(w1, b1, w2, b2):
            h = jax.nn.relu(x_flat @ w1 + b1)
            return jax.nn.relu(h @ w2 + b2)
        y_all = jax.vmap(expert_mlp)(weights1, bias1, weights2, bias2)
        out_flat = y_all[routed_idx, jnp.arange(n)]
        return out_flat.reshape(b, k, d)
    x = x + _L0_attn_ref(_layernorm(x, axis=-1), L0_attn_wq, L0_attn_wk_down, L0_attn_wv_down, L0_attn_wk_up, L0_attn_wv_up, L0_attn_wo)
    x = x + _L0_xattn_ref(_layernorm(x, axis=-1), ctx_1024, L0_xattn_w_q, L0_xattn_w_k, L0_xattn_w_v, L0_xattn_w_o)
    x = x + _L0_ffn_ref(_layernorm(x, axis=-1), L0_ffn_gate_w, L0_ffn_w1, L0_ffn_w2)
    x = x + _L1_attn_ref(_layernorm(x, axis=-1), L1_attn_Wq, L1_attn_bq, L1_attn_Wk, L1_attn_bk, L1_attn_Wv, L1_attn_bv, L1_attn_Wc2q, L1_attn_bc2q, L1_attn_Wo, L1_attn_bo, L1_attn_g1, L1_attn_beta1, L1_attn_g2, L1_attn_beta2, L1_attn_W1, L1_attn_b1, L1_attn_Wm, L1_attn_bm, L1_attn_Wqo, L1_attn_bqo, L1_attn_W2, L1_attn_b2)
    x = x + _L1_xattn_ref(_layernorm(x, axis=-1), ctx_1024, L1_xattn_Wq, L1_xattn_bq, L1_xattn_Wk, L1_xattn_bk, L1_xattn_Wv, L1_xattn_bv, L1_xattn_Wo, L1_xattn_bo)
    x = x + _L1_ffn_ref(_layernorm(x, axis=-1), L1_ffn_gate_query, L1_ffn_log_temp, L1_ffn_w1, L1_ffn_b1, L1_ffn_w2, L1_ffn_b2)
    x = x + _L2_attn_ref(_layernorm(x, axis=-1), L2_attn_Wq, L2_attn_Wkv, L2_attn_Wo, L2_attn_bo)
    x = x + _L2_xattn_ref(_layernorm(x, axis=-1), ctx_1024, ctx_1024, mask_BxSxS2_ik1, L2_xattn_Wq, L2_xattn_bq, L2_xattn_Wk, L2_xattn_bk, L2_xattn_Wv, L2_xattn_bv)
    x = x + _L2_ffn_ref(_layernorm(x, axis=-1), L2_ffn_gate_w, L2_ffn_expert_gate, L2_ffn_expert_up, L2_ffn_expert_down, L2_ffn_shared_gate, L2_ffn_shared_up, L2_ffn_shared_down)
    x = x + _L3_attn_ref(_layernorm(x, axis=-1), L3_attn_Wa, L3_attn_Wout_w, L3_attn_Wout_b)
    x = x + _L3_xattn_ref(_layernorm(x, axis=-1), ctx_1024, ctx_1024, mask_SxS2_ik0, L3_xattn_Wq, L3_xattn_bq, L3_xattn_Wk, L3_xattn_bk, L3_xattn_Wv, L3_xattn_bv, L3_xattn_Wo, L3_xattn_bo)
    x = x + _L3_ffn_ref(_layernorm(x, axis=-1), L3_ffn_router_w, L3_ffn_router_b, L3_ffn_weights1, L3_ffn_bias1, L3_ffn_weights2, L3_ffn_bias2)
    return x

_drawn_inputs = setup_inputs


def setup_inputs(seed=0):
    import zlib

    import numpy as np

    out = dict(_drawn_inputs(seed))
    spreads = {'L1_attn_bq': (0.0, 0.8),
     'L1_attn_bk': (0.0, 2.0),
     'L1_attn_bv': (0.0, 0.429),
     'L1_attn_bc2q': (0.0, 2.0),
     'L1_attn_bo': (0.0, 0.1),
     'L1_attn_g1': (1.0, 0.2),
     'L1_attn_beta1': (0.0, 0.1),
     'L1_attn_g2': (1.0, 0.2),
     'L1_attn_beta2': (0.0, 0.1),
     'L1_attn_b1': (0.0, 0.8),
     'L1_attn_bm': (0.0, 0.8),
     'L1_attn_bqo': (0.0, 0.291),
     'L1_attn_b2': (0.0, 0.1),
     'L1_xattn_bq': (0.0, 0.8),
     'L1_xattn_bk': (0.0, 2.0),
     'L1_xattn_bv': (0.0, 0.505),
     'L1_xattn_bo': (0.0, 0.1),
     'L1_ffn_b1': (0.0, 0.8),
     'L1_ffn_b2': (0.0, 0.8),
     'L2_attn_bo': (0.0, 0.1),
     'L2_xattn_bq': (0.0, 0.8),
     'L2_xattn_bk': (0.0, 2.0),
     'L2_xattn_bv': (0.0, 0.1)}
    factors = {'L1_attn_Wq': 8.0,
     'L1_attn_Wk': 8.0,
     'L1_attn_Wv': 3.461,
     'L1_attn_Wc2q': 8.0,
     'L1_attn_Wo': 2.68,
     'L1_attn_W1': 8.0,
     'L1_attn_Wm': 8.0,
     'L1_attn_Wqo': 8.0,
     'L1_xattn_Wq': 8.0,
     'L1_xattn_Wk': 8.0,
     'L1_xattn_Wv': 3.134,
     'L1_ffn_gate_query': 5.443,
     'L1_ffn_w1': 5.905,
     'L1_ffn_w2': 5.426,
     'L2_xattn_Wq': 3.171,
     'L2_xattn_Wk': 2.941,
     'L2_ffn_gate_w': 8.0,
     'L2_ffn_expert_gate': 8.0,
     'L2_ffn_expert_up': 8.0,
     'L2_ffn_expert_down': 8.0,
     'L2_ffn_shared_gate': 8.0,
     'L2_ffn_shared_up': 8.0,
     'L2_ffn_shared_down': 8.0,
     'L3_attn_Wout_b': 23.441,
     'L3_xattn_Wq': 8.0,
     'L3_xattn_bq': 38.953,
     'L3_xattn_Wk': 8.0,
     'L3_xattn_bk': 64.0,
     'L3_xattn_Wv': 4.762,
     'L3_xattn_bv': 8.0,
     'L3_xattn_Wo': 4.788,
     'L3_xattn_bo': 21.506,
     'L3_ffn_bias1': 41.76,
     'L3_ffn_bias2': 15.444,
     'L3_attn_Wa': 7.898,
     'L3_attn_Wout_w': 8.0,
     'L3_ffn_router_b': 6.327,
     'L3_ffn_weights1': 3.84,
     'L3_ffn_weights2': 2.842}
    for name, (base, spread) in spreads.items():
        noise = np.random.default_rng([zlib.crc32(name.encode()), seed]).standard_normal(out[name].shape)
        drawn = base * np.exp(spread * noise) if base else spread * noise
        out[name] = jnp.asarray(drawn.astype(out[name].dtype))
    for name, factor in factors.items():
        out[name] = (out[name] * factor).astype(out[name].dtype)
    return out
```

```python
import concourse.bass as bass
from concourse import mybir
from concourse.alu_op_type import AluOpType as ALU
from contextlib import ExitStack
import numpy as np

F32 = mybir.dt.float32
BF16 = mybir.dt.bfloat16
I32 = mybir.dt.int32
U32 = mybir.dt.uint32
ACT = mybir.ActivationFunctionType
AX = mybir.AxisListType.X

P = 128
B = 8
S = 256
QT = S // P
NT = B * QT
KX = 512
EPS = 1e-5
RING = 8
BANK = 512
MASKED_FINITE = -1e9
MASKED = -1e30


class Step:

    def __init__(self, sem, per_pass):
        self.sem, self.per_pass = sem, per_pass

    def after(self, b, k):
        return b * self.per_pass + (k + 1)


def wait_step(eng, step, b, k):
    eng.wait_ge(step.sem, step.after(b, k))


class Semaphores:

    def __init__(self, nc, ctx, prefix):
        self.nc, self.ctx, self.prefix, self.used, self.steps = nc, ctx, prefix, [], []

    def __call__(self, name):
        self.used.append(self.ctx.enter_context(self.nc.semaphore(self.prefix + name)))
        return self.used[-1]

    def step(self, name, per_pass):
        self.steps.append(Step(self(name), per_pass))
        return self.steps[-1]

    def start(self, eng):
        for step in self.steps:
            eng.sem_inc(step.sem, 1)

    def clear(self):
        numbers = sorted(s.num for s in self.used)
        runs = []
        for n in numbers:
            if runs and runs[-1][1] == n:
                runs[-1][1] = n + 1
            else:
                runs.append([n, n + 1])
        with self.nc.Block() as block:

            @block.sync
            def _(sp):
                for first, end in runs:
                    sp.sem_clear(range(first, end))


def attention(nc, x_sb, const, w, cfg):
    H, hd, nkeys = cfg["heads"], cfg["hd"], cfg["nkeys"]
    causal, cross, rope = cfg.get("causal"), cfg.get("cross"), cfg.get("rope")
    masked, latent = cfg.get("masked"), cfg.get("latent")
    mask_each = cfg.get("mask_each")
    masked = masked or mask_each
    qk_bias, out_bias = cfg.get("qk_bias"), cfg.get("out_bias")
    scale = cfg["scale"]
    nqc = H * hd // P
    hpc = P // hd
    nkc = cfg["kchunks"]
    nkt = nkeys // P
    vcols = cfg["vcols"]
    small = hd < 32
    gh = 4 if small else hpc
    groups = H // gh
    hpu = 1 if nkeys == KX else 2
    units = H // hpu
    if causal:
        pieces = [(0, 0, 0, S), (S, 1, P, P)]
    else:
        pieces = [(S * t, t, 0, S) for t in range(nkt)]
    hcols = 2 * BANK // hpu
    used = sum(p[3] for p in pieces)
    last_unit = lambda g: ((g + 1) * gh - 1) // hpu

    with ExitStack() as ctx:
        sb = lambda n, s, d=F32: ctx.enter_context(nc.sbuf_tensor(cfg["name"] + n, s, d))
        ps = lambda n, s, d=F32: ctx.enter_context(nc.psum_tensor(cfg["name"] + n, s, d))
        sem = Semaphores(nc, ctx, cfg["name"])

        w_q = sb("w_q", [P, nqc * P])
        w_k = sb("w_k", [P, 64 if latent else nkc * P])
        w_v = sb("w_v", [P, 64 if latent else vcols])
        w_o = sb("w_o", [P, groups, P])
        if rope:
            w_qr = sb("w_qr", [P, nqc * P])
            w_kr = sb("w_kr", [P, nkc * P])
            cos_sin = sb("cos_sin", [P, 2, S])
            turned = sb("turned", [P, 2, 2, S])
        if latent:
            k_up = sb("k_up", [64, nkc, P])
            v_up = sb("v_up", [64, vcols])
            lat = sb("lat", [64, 2, S])
        if qk_bias:
            b_q = sb("b_q", [P, 1])
            b_k = sb("b_k", [P, 1])
            b_v = sb("b_v", [P, P])
        if out_bias:
            b_o = sb("b_o", [P, P])
        if masked:
            mask_q = sb("mask_q", [P, QT, KX], BF16)
            mask_k = sb("mask_k", [P, 2, nkt, S], BF16)
            mask_in = sb("mask_in", [P, 2 if mask_each else 1, 1024], I32)
        if mask_each:
            row_max = sb("row_max", [P, QT])
            some = sb("some", [P, QT])
            some_diag = sb("some_diag", [P, QT, P], BF16)
            some_row = sb("some_row", [P, S])
        stats = sb("stats", [P, QT, 6])
        mean_var = sb("mean_var", [P, QT, 2])
        rstd = sb("rstd", [P, QT])
        fill = sb("fill", [P, 1])
        xn = sb("xn", [P, QT, P])
        xT = sb("xT", [P, S])
        src = sb("src", [P, KX]) if cross else xT
        if small:
            whole = {"q": sb("q_whole", [P, S]), "k": sb("k_whole", [P, nkeys])}
            rest = {"q": sb("q_rest", [P, S]), "k": sb("k_rest", [P, nkeys])}
            parts = {"q": sb("q_parts", [P, 3, S], BF16), "k": sb("k_parts", [P, 3, nkeys], BF16)}
            q_dram = nc.dram_tensor(cfg["name"] + "q_dram", [5, P, S], BF16)
            k_dram = nc.dram_tensor(cfg["name"] + "k_dram", [3, P, nkeys], BF16)
            q_stack = sb("q_stack", [P, 2, H, S], BF16)
            k_stack = sb("k_stack", [P, 2, H, nkeys], BF16)
        else:
            qm = sb("qm", [P, 2, H, S])
            kT = sb("kT", [P, 2, nkc, nkeys])
        v = sb("v", [P, 2, nkt, H, 32]) if small else sb("v", [P, 2, nkt, vcols])
        mx = sb("mx", [P, QT, H])
        mrest = sb("mrest", [P, 2, QT, H])
        mparts = sb("mparts", [P, QT, 8, 16], BF16)
        m_rows = sb("m_rows", [P, 2, S], BF16)
        p_ring = sb("p_ring", [P, RING, 2 * BANK])
        sums = sb("sums", [P, 2, S])
        oT = sb("oT", [P, groups, S])

        ps_ring = ps("ps_ring", [P, 2, BANK])
        ps_t = ps("ps_t", [P, 2, 2 * BANK])
        ps_o = ps("ps_o", [P, 2, 2, S])

        weights = sem("weights")
        n_ready = 5 if small else 3
        ready = sem("ready")
        items = [("x", None, "act")]
        if mask_each:
            items += [("some", 0, "act")]
        if latent:
            items += [("lat", 0, "act")]
        if small:
            items += [("q8", 0, "act")]
        else:
            for c in range(nqc):
                items += [("q", c, "dve" if rope or mask_each else "act")]
        for c in range(nkc):
            items += [("k", c, "dve" if rope else "act")]
        vblk = max(1, nkt * vcols // BANK)
        for c in range(vblk):
            items += [("v", c, "dve" if qk_bias else "act")]
        first_s = len(items)
        for h in range(H):
            if hpu == 2:
                items += [("s", (h, None), "dve")]
            else:
                items += [("s", (h, 0), "dve"), ("s", (h, 1), "dve")]
        items += [("m", None, "dve")]
        n_act = sum(i[2] == "act" for i in items)
        n_dve = sum(i[2] == "dve" for i in items)
        ring_full = sem.step("ring_full", len(items))
        act_took = sem.step("act_took", n_act)
        dve_took = sem.step("dve_took", n_dve)
        took = {"act": act_took, "dve": dve_took}
        order = {}
        seen = {"act": 0, "dve": 0}
        for n, it in enumerate(items):
            seen[it[2]] += 1
            order[n] = seen[it[2]]
        last_of = {}
        for n, it in enumerate(items):
            last_of[it[0]] = (it[2], order[n])

        src_loaded = sem.step("src_loaded", 16)
        ln_done = sem.step("ln_done", 3 * QT + 1)
        ln_pool = sem.step("ln_pool", 1)
        qm_done = sem.step("qm_done", H)
        if small:
            q_split = sem.step("q_split", 4)
            k_split = sem.step("k_split", 4)
            q_stored = sem.step("q_stored", 32)
            k_stored = sem.step("k_stored", 16)
            q_stacked = sem.step("q_stacked", 48)
            k_stacked = sem.step("k_stacked", 48)
        k_turned = sem.step("k_turned", 2 * nkc)
        v_added = sem.step("v_added", nkt)
        masks_in = sem.step("masks_in", 16)
        mask_steps = sem.step("mask_steps", 4 + QT)
        m_steps = sem.step("m_steps", 5)
        t_full = sem.step("t_full", units)
        exp_done = sem.step("exp_done", units)
        pv_done = sem.step("pv_done", groups)
        per_sum = 2 if small else 1
        sum_steps = sem.step("sum_steps", per_sum * groups)
        o_done = sem.step("o_done", groups)
        y_full = sem.step("y_full", 1)
        x_done = sem.step("x_done", QT * (2 if out_bias else 1))

        loads = [(w_q[:], w["w_q"]), (w_k[:], w["w_k"]), (w_v[:], w["w_v"]), (w_o[:], w["w_o"])]
        if rope:
            loads += [(w_qr[:], w["w_qr"]), (w_kr[:], w["w_kr"]), (cos_sin[:], w["cos_sin"])]
        if latent:
            loads += [(k_up[:], w["k_up"]), (v_up[:], w["v_up"])]
        if qk_bias:
            loads += [(b_q[:], w["b_q"]), (b_k[:], w["b_k"]), (b_v[:], w["b_v"].broadcast_to([P, P]))]
        if out_bias:
            loads += [(b_o[:], w["b_o"].broadcast_to([P, P]))]
        nloads = 16 * len(loads)
        mask_loaded = sem("mask_loaded")
        mask_made = sem("mask_made")

        def ring(n, par):
            return ps_ring[:, (par * len(items) + n) % 2, :]

        def outputs(g, par):
            return ps_o[:, (par * (groups + 1) + g) % 2]

        def two_back(eng, step, b):
            if not (isinstance(b, int) and b == 0):
                wait_step(eng, step, b - 1, 0)

        front = [("ln", 0)]
        for n, it in enumerate(items):
            if n == first_s and small:
                front.append(("split", 0))
            if it[0] == "m":
                front.append(("negate", 0))
            front.append(("item", n))
        rear, g = [], 0
        for u in range(units + 3):
            if u < units:
                rear.append(("scores", u))
            if u == 1:
                rear.append(("project", 0))
            while g < groups and last_unit(g) + 2 <= u:
                rear.append(("values", g))
                g += 1
        both = []
        for i, (kind, k) in enumerate(rear):
            both.append((kind, k, -1 if kind == "project" else 0))
            places = max(1, len(rear) * 9 // 10)
            both += [(f[0], f[1], 1) for j, f in enumerate(front) if min(j * places // len(front), len(rear) - 1) == i]

        def passes(eng, emit):
            for kind, k in front:
                emit(kind, k, 0, 0)
            for kind, k, off in both:
                if off >= 0:
                    emit(kind, k, off, off)
            with eng.Fori(0, (B - 2) // 2) as i:
                for c in (1, 2):
                    for kind, k, off in both:
                        emit(kind, k, i * 2 + (c + off), (c + off) % 2)
            for kind, k, off in both:
                if off <= 0:
                    emit(kind, k, B - 1 + off, (B - 1 + off) % 2)
            emit("project", 0, B - 1, (B - 1) % 2)


        def split(eng, name, steps, b):
            x, r, part = whole[name], rest[name], parts[name]
            zero = const["zero"][:].broadcast_to(list(x.shape))
            eng.tensor_tensor(part[:, 0, :], x[:], zero, ALU.add).then_inc(steps.sem, 1)
            wait_step(eng, steps, b, 1)
            eng.tensor_tensor(r[:], x[:], part[:, 0, :], ALU.subtract).then_inc(steps.sem, 1)
            wait_step(eng, steps, b, 2)
            eng.tensor_tensor(part[:, 1, :], r[:], zero, ALU.add).then_inc(steps.sem, 1)
            wait_step(eng, steps, b, 3)
            eng.tensor_tensor(part[:, 2, :], r[:], part[:, 1, :], ALU.subtract).then_inc(steps.sem, 1)

        with nc.Block() as block:

            @block.sync
            def _(sp):
                sem.start(sp)
                for dst, s in loads:
                    sp.dma_start(dst, s).then_inc(weights, 16)
                if masked and not mask_each:
                    sp.dma_start(mask_in[:, 0, :], w["mask_q"]).then_inc(mask_loaded, 16)
                    sp.wait_ge(mask_made, 1)
                    sp.dma_start(mask_in[:, 0, :], w["mask_k"]).then_inc(mask_loaded, 16)
                if small:
                    sp.wait_ge(ready, n_ready)

                def step(kind, k, b, par):
                    if kind == "ln" and cross:
                        wait_step(sp, took[last_of["v"][0]], b, 0)
                        sp.dma_start(src[:], w["ctxT"][bass.ds(b, 1)].rearrange("a p k -> p (a k)")).then_inc(
                            src_loaded.sem, 16)
                        if mask_each:
                            wait_step(sp, mask_steps, b, 0)
                            sp.dma_start(mask_in[:], w["masks"][bass.ds(b, 1)].rearrange("a p m k -> p (a m) k")).then_inc(
                                masks_in.sem, 16)
                    if kind == "split":
                        wait_step(sp, q_split, b, 4)
                        sp.dma_start(q_dram[0:3].rearrange("i p k -> p i k"), parts["q"][:]).then_inc(q_stored.sem, 16)
                        sp.dma_start(q_dram[3:5].rearrange("i p k -> p i k"), parts["q"][:, 0:2, :]).then_inc(
                            q_stored.sem, 16)
                        wait_step(sp, k_split, b, 4)
                        sp.dma_start(k_dram[:].rearrange("i p k -> p i k"), parts["k"][:]).then_inc(k_stored.sem, 16)
                        wait_step(sp, q_stored, b, 32)
                        for a in range(3):
                            sp.dma_start(q_stack[24 * a:24 * a + 24, par],
                                         q_dram[a:a + 3].rearrange("i (d h) k -> (i d) h k", h=H)
                                         ).then_inc(q_stacked.sem, 16)
                        wait_step(sp, k_stored, b, 16)
                        for a in range(3):
                            sp.dma_start(k_stack[24 * a:24 * a + 24, par],
                                         k_dram[:].rearrange("i (d h) k -> (i d) h k", h=H)
                                         ).then_inc(k_stacked.sem, 16)

                if cross:
                    passes(sp, step)

            @block.gpsimd
            def _(pool):
                pool.memset(m_rows[:], 0.0).then_inc(ready, 1)
                pool.memset(mparts[:], 0.0).then_inc(ready, 1)
                if small:
                    pool.memset(v[:], 1.0).then_inc(ready, 1)
                    pool.memset(q_stack[:], 0.0).then_inc(ready, 1)
                    pool.memset(k_stack[:], 0.0).then_inc(ready, 1)
                else:
                    pool.memset(qm[:], 0.0).then_inc(ready, 1)
                pool.wait_ge(ready, n_ready)
                if rope:
                    pool.wait_ge(weights, nloads)

                def step(kind, k, b, par):
                    if kind == "ln":
                        wait_step(pool, ln_done, b, QT * 2 + 1)
                        pool.tensor_tensor(rstd[:], mean_var[:, :, 1], const["minus_half"][:, 0:QT],
                                           ALU.pow).then_inc(ln_pool.sem, 1)
                    if kind == "split":
                        wait_step(pool, act_took, b, order[[i[0] for i in items].index("k")])
                        wait_step(pool, k_stored, b, 0)
                        two_back(pool, t_full, b)
                        split(pool, "k", k_split, b)
                    if kind == "item" and rope and items[k][0] in "qk":
                        if k == 1:
                            two_back(pool, t_full, b)
                        wait_step(pool, dve_took, b, order[k])
                        for j in range(2):
                            r = slice(64 * j, 64 * j + 64)
                            is_q = items[k][0] == "q"
                            out = qm[r, par, cfg["pairs"][items[k][1]][j], :] if is_q else kT[r, par, items[k][1], :]
                            pool.tensor_tensor(out, turned[r, k % 2, 0, :], turned[r, k % 2, 1, :],
                                               ALU.add).then_inc((qm_done if is_q else k_turned).sem, 1)

                passes(pool, step)

            @block.vector
            def _(dve):
                dve.wait_ge(ready, n_ready)
                if out_bias or rope or qk_bias:
                    dve.wait_ge(weights, nloads)
                if masked and not mask_each:
                    dve.wait_ge(mask_loaded, 16)
                    dve.tensor_scalar(mask_q[:].rearrange("p a b -> p (a b)"), mask_in[:, 0, :], 0.0, MASKED,
                                      ALU.is_equal, ALU.mult).then_inc(mask_made, 1)
                    dve.wait_ge(mask_loaded, 32)
                    dve.tensor_scalar(mask_k[:, 0].rearrange("p a b -> p (a b)"), mask_in[:, 0, :], 0.0, MASKED,
                                      ALU.is_equal, ALU.mult).then_inc(mask_made, 1)

                def step(kind, k, b, par):
                    if kind == "ln":
                        for t in range(QT):
                            dve.bn_stats(stats[:, t, :], x_sb[:, bass.ds(b * QT + t, 1), :]).then_inc(ln_done.sem, 1)
                        wait_step(dve, ln_done, b, QT)
                        dve.memset(fill[:], 0.0)
                        for t in range(QT):
                            dve.bn_aggr(mean_var[:, t, :], stats[:, t, :]).then_inc(ln_done.sem, 1)
                        wait_step(dve, ln_done, b, 2 * QT)
                        dve.tensor_scalar(mean_var[:, :, 1], mean_var[:, :, 1], EPS, None, ALU.add).then_inc(ln_done.sem, 1)
                        wait_step(dve, ln_pool, b, 1)
                        wait_step(dve, ring_full, b, 0)
                        for t in range(QT):
                            dve.tensor_scalar(xn[:, t, :], x_sb[:, bass.ds(b * QT + t, 1), :], mean_var[:, t, 0:1],
                                              rstd[:, t:t + 1], ALU.subtract, ALU.mult).then_inc(ln_done.sem, 1)
                        if mask_each:
                            wait_step(dve, masks_in, b, 16)
                            two_back(dve, t_full, b)
                            for m, dst in enumerate((mask_q[:], mask_k[:, par])):
                                dve.tensor_scalar(dst.rearrange("p a b -> p (a b)"), mask_in[:, m, :], 1.0, MASKED_FINITE,
                                                  ALU.is_equal, ALU.mult).then_inc(mask_steps.sem, 1)
                            wait_step(dve, mask_steps, b, 2)
                            dve.tensor_reduce(row_max[:], mask_q[:], AX, ALU.max).then_inc(mask_steps.sem, 1)
                            wait_step(dve, mask_steps, b, 3)
                            dve.tensor_scalar(some[:], row_max[:], 0.5 * MASKED_FINITE, None, ALU.is_gt).then_inc(mask_steps.sem, 1)
                            wait_step(dve, mask_steps, b, 4)
                            for t in range(QT):
                                dve.tensor_scalar(some_diag[:, t, :], const["ident_bf"][:], some[:, t:t + 1], None,
                                                  ALU.mult).then_inc(mask_steps.sem, 1)
                    if kind == "split":
                        wait_step(dve, act_took, b, order[[i[0] for i in items].index("q8")])
                        wait_step(dve, q_stored, b, 0)
                        two_back(dve, t_full, b)
                        split(dve, "q", q_split, b)
                    if kind == "item" and items[k][2] == "dve":
                        n, it = k, items[k]
                        kind, a = it[0], it[1]
                        bank = ring(n, par)
                        wait_step(dve, ring_full, b, n + 1)
                        if kind == "q" and mask_each:
                            wait_step(dve, act_took, b, 2)
                            two_back(dve, t_full, b)
                            dve.scalar_tensor_tensor(qm[:, par, 0, :], bank[:, 0:S], b_q[:], some_row[:], ALU.add,
                                                     ALU.mult).then_inc(dve_took.sem, 1)
                        elif kind in ("q", "k"):
                            if kind == "q" and a >= 2:
                                wait_step(dve, qm_done, b, 2 * (a - 1))
                            elif kind == "q":
                                wait_step(dve, k_turned, b, 0)
                            elif a >= 2:
                                wait_step(dve, k_turned, b, 2 * (a - 1))
                            else:
                                wait_step(dve, qm_done, b, 2 * (nqc - 1 + a))
                            dve.tensor_tensor(turned[:, n % 2], bank.rearrange("p (a s) -> p a s", a=2), cos_sin[:],
                                              ALU.mult).then_inc(dve_took.sem, 1)
                        elif kind == "v":
                            two_back(dve, pv_done, b)
                            for t in range(nkt):
                                if not small:
                                    last = dve.tensor_tensor(v[:, par, t, :], bank[:, t * P:(t + 1) * P], b_v[:], ALU.add)
                                    continue
                                last = dve.tensor_tensor(v[:, par, t, :, 0:hd],
                                                         bank[:, t * P:(t + 1) * P].rearrange("p (h d) -> p h d", h=H),
                                                         b_v[:].rearrange("p (h d) -> p h d", h=H), ALU.add)
                            last.then_inc(dve_took.sem, 1)
                        elif kind == "m":
                            two_back(dve, t_full, b)
                            dve.tensor_copy(m_rows[:, par, :], bank.bitcast(BF16)[:, 0:S]).then_inc(dve_took.sem, 1)
                        else:
                            h, qt = a
                            if n <= first_s + 1:
                                wait_step(dve, m_steps, b, 0)
                            if qt is not None:
                                dve.tensor_reduce(mx[:, qt, h:h + 1], bank, AX, ALU.max).then_inc(dve_took.sem, 1)
                            elif causal:
                                dve.tensor_reduce(mx[:, 0, h:h + 1], bank[:, 0:P], AX, ALU.max)
                                dve.tensor_reduce(mx[:, 1, h:h + 1], bank[:, S:2 * S], AX, ALU.max).then_inc(
                                    dve_took.sem, 1)
                            else:
                                dve.tensor_reduce(mx[:, :, h], bank.rearrange("p (q k) -> p q k", q=QT), AX,
                                                  ALU.max).then_inc(dve_took.sem, 1)
                    if kind == "negate":
                        wait_step(dve, dve_took, b, n_dve - 1)
                        wait_step(dve, ring_full, b, 0)
                        dve.tensor_scalar(mparts[:, :, 0, 0:H], mx[:], -1.0, None, ALU.mult).then_inc(m_steps.sem, 1)
                        wait_step(dve, m_steps, b, 1)
                        dve.scalar_tensor_tensor(mrest[:, 0], mx[:], -1.0, mparts[:, :, 0, 0:H], ALU.mult,
                                                 ALU.subtract).then_inc(m_steps.sem, 1)
                        wait_step(dve, m_steps, b, 2)
                        dve.tensor_copy(mparts[:, :, 1, 0:H], mrest[:, 0]).then_inc(m_steps.sem, 1)
                        wait_step(dve, m_steps, b, 3)
                        dve.tensor_tensor(mrest[:, 1], mrest[:, 0], mparts[:, :, 1, 0:H], ALU.subtract).then_inc(m_steps.sem, 1)
                        wait_step(dve, m_steps, b, 4)
                        dve.tensor_copy(mparts[:, :, 2, 0:H], mrest[:, 1]).then_inc(m_steps.sem, 1)
                    if kind == "values":
                        g, o = k, outputs(k, par)
                        wait_step(dve, pv_done, b, g + 1)
                        if small:
                            dve.memset(fill[:], 0.0)
                            dve.stream_shuffle(sums[:, g % 2, :], o[:, 0, :], [hd] * 32).then_inc(sum_steps.sem, 1)
                            wait_step(dve, sum_steps, b, 2 * g + 1)
                            dve.reciprocal(sums[:, g % 2, :], sums[:, g % 2, :]).then_inc(sum_steps.sem, 1)
                        else:
                            dve.reciprocal(sums[:, g % 2, :], o[:, 1, :]).then_inc(sum_steps.sem, 1)
                        wait_step(dve, sum_steps, b, per_sum * (g + 1))
                        if g == 0:
                            wait_step(dve, y_full, b, 0)
                        dve.tensor_tensor(oT[:, g, :], o[:, 0, :], sums[:, g % 2, :], ALU.mult).then_inc(o_done.sem, 1)
                    if kind == "project":
                        wait_step(dve, y_full, b, 1)
                        for t in range(QT):
                            dve.tensor_tensor(x_sb[:, bass.ds(b * QT + t, 1), :], x_sb[:, bass.ds(b * QT + t, 1), :],
                                              outputs(groups, par)[:, 0, t * P:(t + 1) * P].rearrange("p (a k) -> p a k", a=1),
                                              ALU.add).then_inc(x_done.sem, 1)
                        if out_bias:
                            wait_step(dve, x_done, b, QT)
                            for t in range(QT):
                                dve.tensor_tensor(x_sb[:, bass.ds(b * QT + t, 1), :], x_sb[:, bass.ds(b * QT + t, 1), :],
                                                  b_o[:].rearrange("p (a k) -> p a k", a=1), ALU.add).then_inc(x_done.sem, 1)

                passes(dve, step)

            @block.scalar
            def _(act):
                act.wait_ge(ready, n_ready)
                act.wait_ge(weights, nloads)

                def step(kind, k, b, par):
                    if kind == "item" and items[k][2] == "act":
                        n, it = k, items[k]
                        kind, a = it[0], it[1]
                        bank = ring(n, par)
                        wait_step(act, ring_full, b, n + 1)
                        if kind == "x":
                            act.activation(xT[:], bank[:, 0:S], ACT.Copy).then_inc(act_took.sem, 1)
                        elif kind == "some":
                            act.activation(some_row[:], bank[:, 0:S], ACT.Copy).then_inc(act_took.sem, 1)
                        elif kind == "lat":
                            act.activation(lat[:], bank[0:64, :].rearrange("p (a s) -> p a s", a=2),
                                           ACT.Copy).then_inc(act_took.sem, 1)
                        elif kind == "q8":
                            wait_step(act, q_split, b, 0)
                            if qk_bias:
                                act.activation(whole["q"][:], bank[:, 0:S], ACT.Identity, bias=b_q[:]).then_inc(
                                    act_took.sem, 1)
                            else:
                                act.activation(whole["q"][:], bank[:, 0:S], ACT.Copy).then_inc(act_took.sem, 1)
                        elif kind == "q":
                            if a == 0:
                                two_back(act, t_full, b)
                            if hpc == 1:
                                last = act.activation(qm[:, par, a, :], bank[:, 0:S], ACT.Copy)
                            else:
                                for j in range(2):
                                    r = slice(64 * j, 64 * j + 64)
                                    last = act.activation(qm[r, par, cfg["pairs"][a][j], :], bank[r, 0:S], ACT.Copy)
                            last.then_inc(act_took.sem, 1)
                        elif kind == "k":
                            if small:
                                wait_step(act, k_split, b, 0)
                            elif a == 0 and mask_each:
                                two_back(act, t_full, b)
                            k_out = whole["k"][:] if small else kT[:, par, a, :]
                            if qk_bias:
                                act.activation(k_out, bank[:, 0:nkeys], ACT.Identity, bias=b_k[:]).then_inc(
                                    act_took.sem, 1)
                            else:
                                act.activation(k_out, bank[:, 0:nkeys], ACT.Copy).then_inc(act_took.sem, 1)
                        elif kind == "v":
                            if a == 0:
                                two_back(act, pv_done, b)
                            if small:
                                act.activation(v[:, par, :, :, 0:hd], bank.rearrange("p (t h d) -> p t h d", t=nkt, h=H),
                                               ACT.Copy).then_inc(act_took.sem, 1)
                            else:
                                act.activation(v[:, par].rearrange("p t c -> p (t c)")[:, a * BANK:(a + 1) * BANK], bank,
                                               ACT.Copy).then_inc(act_took.sem, 1)
                    if kind == "scores":
                        u = k
                        wait_step(act, t_full, b, u + 1)
                        if u >= 8:
                            wait_step(act, pv_done, b, ((u - 7) * hpu - 1) // gh + 1)
                        elif u == 0:
                            wait_step(act, pv_done, b, 0)
                        pt = ps_t[:, u % 2, :].rearrange("p (h c) -> p h c", h=hpu)[:, :, 0:used]
                        pr = p_ring[:, u % RING, :].rearrange("p (h c) -> p h c", h=hpu)[:, :, 0:used]
                        act.activation(pr, pt, ACT.Exp, scale=scale).then_inc(exp_done.sem, 1)

                passes(act, step)

            @block.tensor
            def _(pe):
                pe.wait_ge(ready, n_ready)
                pe.wait_ge(weights, nloads)
                if masked and not mask_each:
                    pe.wait_ge(mask_made, 2)

                def step(kind, k, b, par):
                    if kind == "item":
                        n, it = k, items[k]
                        kind, a = it[0], it[1]
                        if n >= 2:
                            wait_step(pe, took[items[n - 2][2]], b, order[n - 2])
                        else:
                            wait_step(pe, dve_took, b, 0)
                        bank = ring(n, par)
                        if kind == "x":
                            wait_step(pe, ln_done, b, 3 * QT + 1)
                            for t in range(QT):
                                last = pe.transpose(bank[:, t * P:(t + 1) * P], xn[:, t, :], const["ident"][:])
                        elif kind == "some":
                            wait_step(pe, mask_steps, b, mask_steps.per_pass)
                            for t in range(QT):
                                last = pe.matmul(bank[:, t * P:(t + 1) * P], const["ones_bf"][:], some_diag[:, t, :],
                                                 start=True, stop=True)
                        elif kind == "lat":
                            wait_step(pe, act_took, b, 1)
                            pe.matmul(bank[0:64, 0:S], w_k[:], xT[:], start=True, stop=True)
                            last = pe.matmul(bank[0:64, S:2 * S], w_v[:], xT[:], start=True, stop=True)
                        elif kind in ("q", "q8"):
                            wait_step(pe, act_took, b, 1)
                            a = a or 0
                            last = pe.matmul(bank[:, 0:S], w_q[:, a * P:(a + 1) * P], xT[:], start=True, stop=True)
                            if rope:
                                last = pe.matmul(bank[:, S:2 * S], w_qr[:, a * P:(a + 1) * P], xT[:], start=True, stop=True)
                        elif kind == "k":
                            if cross:
                                wait_step(pe, src_loaded, b, 16)
                            if latent:
                                wait_step(pe, act_took, b, 2)
                                last = pe.matmul(bank[:, 0:S], k_up[:, a, :], lat[:, 0, :], start=True, stop=True)
                            else:
                                last = pe.matmul(bank[:, 0:nkeys], w_k[:, a * P:(a + 1) * P], src[:], start=True, stop=True)
                                if rope:
                                    last = pe.matmul(bank[:, S:2 * S], w_kr[:, a * P:(a + 1) * P], src[:], start=True,
                                                     stop=True)
                        elif kind == "v":
                            width = min(BANK, vcols)
                            for j in range(BANK // width):
                                col = a * BANK + j * width
                                t, c0 = col // vcols, col % vcols
                                out = bank[:, j * width:(j + 1) * width]
                                if latent:
                                    last = pe.matmul(out, lat[:, 1, t * P:(t + 1) * P], v_up[:, c0:c0 + width], start=True,
                                                     stop=True)
                                else:
                                    last = pe.matmul(out, src[:, t * P:(t + 1) * P], w_v[:, c0:c0 + width], start=True,
                                                     stop=True)
                        elif kind == "m":
                            wait_step(pe, m_steps, b, 5)
                            for t in range(QT):
                                last = pe.transpose(bank.bitcast(BF16)[:, t * P:(t + 1) * P],
                                                    mparts[:, t, :, :].rearrange("p a h -> p (a h)"), const["ident_bf"][:])
                        else:
                            h, qt = a
                            if n == first_s:
                                if n_act:
                                    wait_step(pe, act_took, b, n_act)
                                if rope:
                                    wait_step(pe, k_turned, b, 2 * nkc)
                                    wait_step(pe, qm_done, b, H)
                            if small and n == first_s:
                                wait_step(pe, k_stacked, b, 48)
                                wait_step(pe, q_stacked, b, 48)
                            queries = q_stack[:, par, h, :] if small else qm[:, par, h, :]
                            keys = k_stack[:, par, h, :] if small else kT[:, par, cfg["kchunk"](h), :]
                            for t in ([qt] if qt is not None else range(QT)):
                                seen_keys = P * (t + 1) if causal else nkeys
                                out = bank[:, 0:seen_keys] if qt is not None else bank[:, S * t:S * t + seen_keys]
                                last = pe.matmul(out, queries[:, t * P:(t + 1) * P], keys[:, 0:seen_keys], start=True,
                                                 stop=not masked)
                                if masked:
                                    last = pe.matmul(out, const["ident_bf"][:], mask_q[:, t, :], start=False, stop=True)
                                if causal:
                                    last = pe.matmul(out[:, seen_keys - P:seen_keys], const["ident_bf"][:],
                                                     const["causal_q"][:], start=False, stop=True, skip_group_check=True)
                        last.then_inc(ring_full.sem, 1)
                    if kind == "scores":
                        u = k
                        if u == 0:
                            wait_step(pe, dve_took, b, n_dve)
                        if u >= 2:
                            wait_step(pe, exp_done, b, u - 1)
                        else:
                            wait_step(pe, exp_done, b, 0)
                        for j in range(hpu):
                            h = u * hpu + j
                            for col, t, q0, nq in pieces:
                                out = ps_t[:, u % 2, j * hcols + col:j * hcols + col + nq]
                                queries = q_stack[:, par, h, :] if small else qm[:, par, h, :]
                                keys = k_stack[:, par, h, :] if small else kT[:, par, cfg["kchunk"](h), :]
                                pe.matmul(out, keys[:, t * P:(t + 1) * P], queries[:, q0:q0 + nq], start=True, stop=False)
                                diag = causal
                                last = pe.matmul(out, const["max_rows"][:, h, :], m_rows[:, par, q0:q0 + nq], start=False,
                                                 stop=not masked)
                                if masked:
                                    last = pe.matmul(out, const["ident_bf"][:], mask_k[:, par if mask_each else 0, t, q0:q0 + nq], start=False, stop=True)
                                if diag:
                                    last = pe.matmul(out[:, 0:P], const["ident_bf"][:], const["causal_k"][:], start=False,
                                                     stop=True, skip_group_check=True)
                        last.then_inc(t_full.sem, 1)
                    if kind == "values":
                        g = k
                        wait_step(pe, exp_done, b, last_unit(g) + 1)
                        if g == 1:
                            wait_step(pe, x_done, b, 0)
                        else:
                            wait_step(pe, o_done, b, max(0, g - 1))
                        for i, (col, t, q0, nq) in enumerate(pieces):
                            for j in range(gh):
                                h = g * gh + j
                                u = h // hpu
                                c0 = (h % hpu) * hcols + col
                                prob = p_ring[:, u % RING, c0:c0 + nq]
                                if small:
                                    val, rows = v[:, par, t, h, :], slice(32 * j, 32 * j + 32)
                                else:
                                    hv = cfg["vhead"](h)
                                    val, rows = v[:, par, t, hv * hd:(hv + 1) * hd], slice(hd * j, hd * j + hd)
                                last = pe.matmul(outputs(g, par)[rows, 0, q0:q0 + nq], val, prob, start=(i == 0),
                                                 stop=(i == len(pieces) - 1), skip_group_check=True)
                        if not small:
                            for i, (col, t, q0, nq) in enumerate(pieces):
                                for j in range(gh):
                                    h = g * gh + j
                                    u = h // hpu
                                    c0 = (h % hpu) * hcols + col
                                    prob = p_ring[:, u % RING, c0:c0 + nq]
                                    last = pe.matmul(outputs(g, par)[hd * j:hd * j + hd, 1, q0:q0 + nq], const["ones"][:, 0:hd], prob,
                                                     start=(i == 0), stop=(i == len(pieces) - 1), skip_group_check=True)
                        last.then_inc(pv_done.sem, 1)
                    if kind == "project":
                        wait_step(pe, o_done, b, groups)
                        if groups == 1:
                            wait_step(pe, x_done, b, 0)
                        for t in range(QT):
                            for g in range(groups):
                                last = pe.matmul(outputs(groups, par)[:, 0, t * P:(t + 1) * P], oT[:, g, t * P:(t + 1) * P],
                                                 w_o[:, g, :], start=(g == 0), stop=(g == groups - 1))
                        last.then_inc(y_full.sem, 1)

                passes(pe, step)
        sem.clear()


def normalize_all(nc, x_sb, xn, xT, const, name, to_dram=None):
    with ExitStack() as ctx:
        sb = lambda n, s, d=F32: ctx.enter_context(nc.sbuf_tensor(name + n, s, d))
        sem = Semaphores(nc, ctx, name)
        stats = sb("stats", [P, NT, 6])
        mean_var = sb("mean_var", [P, NT, 2])
        rstd = sb("rstd", [P, NT])
        if xT is not None:
            ps_x = ctx.enter_context(nc.psum_tensor(name + "ps_x", [P, 4, BANK], F32))
        stat_steps, powered, normed = sem("stat_steps"), sem("powered"), sem("normed")
        turned, copied, stored = sem("turned"), sem("copied"), sem("stored")
        with nc.Block() as block:

            @block.vector
            def _(dve):
                for t in range(NT):
                    dve.bn_stats(stats[:, t, :], x_sb[:, t, :]).then_inc(stat_steps, 1)
                for t in range(NT):
                    dve.wait_ge(stat_steps, t + 1)
                    dve.bn_aggr(mean_var[:, t, :], stats[:, t, :]).then_inc(stat_steps, 1)
                dve.wait_ge(stat_steps, 2 * NT)
                dve.tensor_scalar(mean_var[:, :, 1], mean_var[:, :, 1], EPS, None, ALU.add).then_inc(stat_steps, 1)
                dve.wait_ge(powered, 1)
                for t in range(NT):
                    dve.tensor_scalar(xn[:, t, :], x_sb[:, t, :], mean_var[:, t, 0:1], rstd[:, t:t + 1], ALU.subtract,
                                      ALU.mult).then_inc(normed, 1)

            @block.gpsimd
            def _(pool):
                pool.wait_ge(stat_steps, 2 * NT + 1)
                pool.tensor_tensor(rstd[:], mean_var[:, :, 1], const["minus_half"][:], ALU.pow).then_inc(powered, 1)

            @block.tensor
            def _(pe):
                for t in range(NT if xT is not None else 0):
                    pe.wait_ge(normed, t + 1)
                    pe.transpose(ps_x[:, t // 4, (t % 4) * P:(t % 4 + 1) * P], xn[:, t, :], const["ident"][:]).then_inc(
                        turned, 1)

            @block.scalar
            def _(act):
                for c in range(4 if xT is not None else 0):
                    act.wait_ge(turned, 4 * (c + 1))
                    act.activation(xT[:, c * BANK:(c + 1) * BANK], ps_x[:, c, :], ACT.Copy).then_inc(copied, 1)

            @block.sync
            def _(sp):
                sem.start(sp)
                if to_dram is not None:
                    for what, dst in to_dram:
                        if what == "xn":
                            sp.wait_ge(normed, NT)
                        s = xn if what == "xn" else x_sb
                        sp.dma_start(dst.rearrange("(t p) d -> p t d", p=P), s[:]).then_inc(stored, 16)
                    sp.wait_ge(stored, 16 * len(to_dram))
        sem.clear()


def ffn_argmax_experts(nc, x_sb, const, w, cfg):
    E, HID = 32, 32
    CH = E * HID // P
    EC = P // HID
    NB = NT * P // BANK
    TB = BANK // P
    with ExitStack() as ctx:
        sb = lambda n, s, d=F32: ctx.enter_context(nc.sbuf_tensor(cfg["name"] + n, s, d))
        sem = Semaphores(nc, ctx, cfg["name"])
        xn = sb("xn", [P, NT, P])
        xT = sb("xT", [P, NT * P])
        normalize_all(nc, x_sb, xn, xT, const, cfg["name"] + "ln_")
        w_r = sb("w_r", [P, E])
        b_r = sb("b_r", [P, E])
        w_1 = sb("w_1", [P, E * HID])
        b_1 = sb("b_1", [P, CH])
        w_2 = sb("w_2", [P, CH, P])
        b_2 = sb("b_2", [P, P])
        logits = sb("logits", [P, NT, E])
        best = sb("best", [P, NT])
        onehot = sb("onehot", [P, NT, E])
        ohT = sb("ohT", [P, NT * P])
        ohTb = sb("ohTb", [P, NT * P], BF16)
        hid = sb("hid", [P, 2, BANK])
        hid_m = sb("hid_m", [P, 2, BANK])
        yT = sb("yT", [P, BANK])
        ps = ctx.enter_context(nc.psum_tensor(cfg["name"] + "ps", [P, 8, BANK], F32))
        loaded, zeroed = sem("loaded"), sem("zeroed")
        logit_full, route, oh_full, oh_out = sem("logit_full"), sem("route"), sem("oh_full"), sem("oh_out")
        h_full, h_relu = sem.step("h_full", CH), sem.step("h_relu", CH)
        m_full, h_masked = sem.step("m_full", CH), sem.step("h_masked", CH)
        y_full, y_relu = sem.step("y_full", CH), sem.step("y_relu", 1)
        t_full, x_done = sem.step("t_full", 1), sem.step("x_done", 1)
        loads = [(w_r[:], w["w_r"]), (b_r[:], w["b_r"].broadcast_to([P, E])), (w_1[:], w["w_1"]), (b_1[:], w["b_1"]),
                 (w_2[:], w["w_2"]), (b_2[:], w["b_2"])]
        LOADED = 16 * len(loads)
        with nc.Block() as block:

            @block.sync
            def _(sp):
                sem.start(sp)
                for dst, s in loads:
                    sp.dma_start(dst, s).then_inc(loaded, 16)

            @block.gpsimd
            def _(pool):
                pool.memset(ohTb[:], 0.0)
                pool.memset(ohT[:], 0.0).then_inc(zeroed, 1)

            @block.vector
            def _(dve):
                dve.wait_ge(loaded, LOADED)
                dve.wait_ge(logit_full, 1)
                dve.tensor_tensor(logits[:], ps[:, 0, :].rearrange("p (t e) -> p t e", t=NT),
                                  b_r[:].rearrange("p (a e) -> p a e", a=1).broadcast_to([P, NT, E]), ALU.add).then_inc(route, 1)
                dve.wait_ge(route, 1)
                dve.tensor_reduce(best[:], logits[:], AX, ALU.max).then_inc(route, 1)
                dve.wait_ge(route, 2)
                spread = best[:].rearrange("p (t a) -> p t a", a=1).broadcast_to([P, NT, E])
                dve.tensor_tensor(logits[:], logits[:], spread, ALU.is_equal).then_inc(route, 1)
                dve.wait_ge(route, 3)
                dve.tensor_tensor(logits[:], logits[:], const["rank_down"][:, 0:E].rearrange("p (a e) -> p a e", a=1).broadcast_to(
                    [P, NT, E]), ALU.mult).then_inc(route, 1)
                dve.wait_ge(route, 4)
                dve.tensor_reduce(best[:], logits[:], AX, ALU.max).then_inc(route, 1)
                dve.wait_ge(route, 5)
                dve.tensor_tensor(onehot[:], logits[:], spread, ALU.is_equal).then_inc(route, 1)
                with dve.Fori(0, NB) as blk:
                    for c in range(CH):
                        wait_step(dve, h_relu, blk, c + 1)
                        wait_step(dve, m_full, blk, c + 1)
                        wait_step(dve, y_full, blk, max(0, c - 1))
                        dve.tensor_tensor(hid_m[:, c % 2, :], hid[:, c % 2, :], ps[:, 2 + c % 2, :], ALU.mult).then_inc(
                            h_masked.sem, 1)
                    wait_step(dve, t_full, blk, 1)
                    tiles = bass.ds(blk * TB, TB)
                    dve.tensor_tensor(x_sb[:, tiles, :], x_sb[:, tiles, :], ps[:, 6, :].rearrange("p (t d) -> p t d", t=TB),
                                      ALU.add).then_inc(x_done.sem, 1)

            @block.scalar
            def _(act):
                act.wait_ge(loaded, LOADED)
                act.wait_ge(zeroed, 1)
                for c in range(NB):
                    act.wait_ge(oh_full, TB * (c + 1))
                    act.activation(ohT[0:E, c * BANK:(c + 1) * BANK], ps[0:E, 4 + c % 2, :], ACT.Copy).then_inc(oh_out, 1)
                    act.activation(ohTb[0:E, c * BANK:(c + 1) * BANK], ps[0:E, 4 + c % 2, :], ACT.Copy).then_inc(oh_out, 1)
                with act.Fori(0, NB) as blk:
                    for c in range(CH):
                        wait_step(act, h_full, blk, c + 1)
                        wait_step(act, h_masked, blk, max(0, c - 1))
                        act.activation(hid[:, c % 2, :], ps[:, c % 2, :], ACT.Relu, bias=b_1[:, c:c + 1]).then_inc(
                            h_relu.sem, 1)
                    wait_step(act, y_full, blk, CH)
                    wait_step(act, t_full, blk, 0)
                    act.activation(yT[:], ps[:, 4, :], ACT.Relu).then_inc(y_relu.sem, 1)

            @block.tensor
            def _(pe):
                pe.wait_ge(loaded, LOADED)
                pe.wait_ge(zeroed, 1)
                for t in range(NT):
                    last = pe.matmul(ps[:, 0, t * E:(t + 1) * E], xT[:, t * P:(t + 1) * P], w_r[:], start=True, stop=True)
                last.then_inc(logit_full, 1)
                pe.wait_ge(route, 6)
                for t in range(NT):
                    if t >= 2 * TB:
                        pe.wait_ge(oh_out, 2 * (t // TB - 1))
                    pe.transpose(ps[0:E, 4 + t // TB % 2, (t % TB) * P:(t % TB + 1) * P], onehot[:, t, :],
                                 const["ident"][:]).then_inc(oh_full, 1)
                pe.wait_ge(oh_out, 2 * NB)
                with pe.Fori(0, NB) as blk:
                    tokens = bass.ds(blk * BANK, BANK)
                    for c in range(CH + 1):
                        if c < CH:
                            wait_step(pe, h_masked, blk, max(0, c - 1))
                            pe.matmul(ps[:, c % 2, :], w_1[:, c * P:(c + 1) * P], xT[:, tokens], start=True,
                                      stop=True).then_inc(h_full.sem, 1)
                            pe.matmul(ps[:, 2 + c % 2, :], const["expert_rows"][:, c, :], ohTb[:, tokens],
                                      start=True, stop=True).then_inc(m_full.sem, 1)
                        if c == 0:
                            wait_step(pe, y_relu, blk, 0)
                            pe.matmul(ps[:, 4, :], b_2[:], ohT[:, tokens], start=True, stop=False)
                        if c >= 1:
                            wait_step(pe, h_masked, blk, c)
                            pe.matmul(ps[:, 4, :], w_2[:, c - 1, :], hid_m[:, (c - 1) % 2, :], start=False,
                                      stop=(c == CH)).then_inc(y_full.sem, 1)
                    wait_step(pe, y_relu, blk, 1)
                    wait_step(pe, x_done, blk, 0)
                    for t in range(TB):
                        last = pe.transpose(ps[:, 6, t * P:(t + 1) * P], yT[:, t * P:(t + 1) * P], const["ident"][:])
                    last.then_inc(t_full.sem, 1)
        sem.clear()


def ffn_dense_experts(nc, x_sb, const, w, cfg):
    E, HID = 8, 352
    parts = [(0, P), (P, P), (2 * P, HID - 2 * P)]
    NB = NT * P // BANK
    TB = BANK // P
    U = E + 1
    with ExitStack() as ctx:
        sb = lambda n, s, d=F32: ctx.enter_context(nc.sbuf_tensor(cfg["name"] + n, s, d))
        sem = Semaphores(nc, ctx, cfg["name"])
        xn = sb("xn", [P, NT, P])
        xT = sb("xT", [P, NT * P])
        normalize_all(nc, x_sb, xn, xT, const, cfg["name"] + "ln_")
        w_r = sb("w_r", [P, E])
        w_g = sb("w_g", [P, U, HID])
        w_u = sb("w_u", [P, U, HID])
        w_d = sb("w_d", [P, U, 3, P])
        logits = sb("logits", [P, NT, E])
        prob = sb("prob", [P, NT, E])
        hot = sb("hot", [P, 2, NT, E])
        top = sb("top", [P, 4, NT])
        comb = sb("comb", [P, NT, E])
        combT = sb("combT", [P, P])
        weight = sb("weight", [P, 2, E, BANK])
        xw = sb("xw", [P, 2, BANK])
        gated = sb("gated", [P, 2, BANK])
        hid = sb("hid", [P, 2, 3, BANK])
        yT = sb("yT", [P, BANK])
        comb_dram = nc.dram_tensor(cfg["name"] + "comb_dram", (NT, E, P), F32, kind="Internal").ap()
        ps = ctx.enter_context(nc.psum_tensor(cfg["name"] + "ps", [P, 8, BANK], F32))
        loaded, logit_full, route, exped = sem("loaded"), sem("logit_full"), sem("route"), sem("exped")
        comb_turned, comb_out, comb_stored = sem("comb_turned"), sem("comb_out"), sem("comb_stored")
        N3 = 3 * U
        w_in = [sem.step("w_in0", 16 * E), sem.step("w_in1", 16 * E)]
        weighted = sem.step("weighted", E)
        g_full, u_full = sem.step("g_full", N3), sem.step("u_full", N3)
        g_out, h_out = sem.step("g_out", N3), sem.step("h_out", N3)
        y_full, y_out = sem.step("y_full", U), sem.step("y_out", 1)
        t_full, x_done = sem.step("t_full", 1), sem.step("x_done", 1)
        loads = [(w_r[:], w["w_r"]), (w_g[:], w["w_g"]), (w_u[:], w["w_u"]), (w_d[:], w["w_d"])]
        LOADED = 16 * len(loads)
        with nc.Block() as block:

            @block.sync
            def _(sp):
                sem.start(sp)
                for dst, s in loads:
                    sp.dma_start(dst, s).then_inc(loaded, 16)
                sp.wait_ge(comb_out, 1)
                sp.dma_start(comb_dram.rearrange("t e p -> (t e) p"), combT[:]).then_inc(comb_stored, 16)
                sp.wait_ge(comb_stored, 16)
                with sp.Fori(0, NB // 2) as pair:
                    for j in range(2):
                        wait_step(sp, weighted, 2 * pair, 0)
                        src = comb_dram[bass.ds((2 * pair + j) * TB, TB)].rearrange("(a t) e p -> a e t p", a=1)
                        for e in range(E):
                            sp.dma_start(weight[:, j, e, :].rearrange("q (t p) -> q t p", t=TB),
                                         src[:, e].broadcast_to([P, TB, P])).then_inc(w_in[j].sem, 16)

            @block.vector
            def _(dve):
                def hidden_products(dve, blk, u):
                    for i, (c0, n) in enumerate(parts):
                        k = 3 * u + i
                        wait_step(dve, g_out, blk, k + 1)
                        wait_step(dve, u_full, blk, k + 1)
                        if i == 0:
                            wait_step(dve, y_full, blk, max(0, u - 1))
                        dve.tensor_tensor(hid[0:n, u % 2, i, :], gated[0:n, k % 2, :], ps[0:n, 2 + k % 2, :], ALU.mult).then_inc(
                            h_out.sem, 1)

                link = [0]

                def chain(ins):
                    link[0] += 1
                    ins.then_inc(route, 1)
                    dve.wait_ge(route, link[0])

                def spread(a):
                    return a.rearrange("p (t a) -> p t a", a=1).broadcast_to([P, NT, E])

                down = const["rank_down"][:, 0:E].rearrange("p (a e) -> p a e", a=1).broadcast_to([P, NT, E])
                dve.wait_ge(logit_full, 1)
                lg = ps[:, 0, 0:NT * E].rearrange("p (t e) -> p t e", t=NT)
                chain(dve.tensor_reduce(top[:, 0], lg, AX, ALU.max))
                chain(dve.tensor_tensor(logits[:], lg, spread(top[:, 0]), ALU.subtract))
                dve.wait_ge(exped, 1)
                chain(dve.tensor_reduce(top[:, 1], prob[:], AX, ALU.add))
                chain(dve.reciprocal(top[:, 1], top[:, 1]))
                chain(dve.tensor_tensor(prob[:], prob[:], spread(top[:, 1]), ALU.mult))
                for k in range(2):
                    chain(dve.tensor_reduce(top[:, 2 + k], prob[:], AX, ALU.max))
                    chain(dve.tensor_tensor(hot[:, k], prob[:], spread(top[:, 2 + k]), ALU.is_equal))
                    chain(dve.tensor_tensor(hot[:, k], hot[:, k], down, ALU.mult))
                    chain(dve.tensor_reduce(top[:, 0], hot[:, k], AX, ALU.max))
                    chain(dve.tensor_tensor(hot[:, k], hot[:, k], spread(top[:, 0]), ALU.is_equal))
                    if k == 0:
                        chain(dve.scalar_tensor_tensor(prob[:].rearrange("p t e -> p (t e)"),
                                                       hot[:, 0].rearrange("p t e -> p (t e)"), -2.0,
                                                       prob[:].rearrange("p t e -> p (t e)"), ALU.mult, ALU.add))
                chain(dve.tensor_tensor(top[:, 0], top[:, 2], top[:, 3], ALU.add))
                chain(dve.tensor_scalar(top[:, 0], top[:, 0], 1e-20, None, ALU.add))
                chain(dve.reciprocal(top[:, 0], top[:, 0]))
                for k in range(2):
                    chain(dve.tensor_tensor(top[:, 2 + k], top[:, 2 + k], top[:, 0], ALU.mult))
                    chain(dve.tensor_tensor(hot[:, k], hot[:, k], spread(top[:, 2 + k]), ALU.mult))
                chain(dve.tensor_tensor(comb[:], hot[:, 0], hot[:, 1], ALU.add))
                with dve.Fori(0, NB // 2) as pair:
                    for j in range(2):
                        blk = 2 * pair + j
                        tokens = bass.ds(blk * BANK, BANK)
                        for u in range(U):
                            if u < E:
                                if u == 0:
                                    wait_step(dve, w_in[j], pair, 16 * E)
                                wait_step(dve, u_full, blk, max(0, 3 * (u - 1)))
                                dve.tensor_tensor(xw[:, u % 2, :], xT[:, tokens], weight[:, j, u, :], ALU.mult).then_inc(
                                    weighted.sem, 1)
                            if u >= 1:
                                hidden_products(dve, blk, u - 1)
                        hidden_products(dve, blk, U - 1)
                        wait_step(dve, t_full, blk, 1)
                        tiles = bass.ds(blk * TB, TB)
                        dve.tensor_tensor(x_sb[:, tiles, :], x_sb[:, tiles, :],
                                          ps[:, 7, :].rearrange("p (t d) -> p t d", t=TB), ALU.add).then_inc(x_done.sem, 1)

            @block.scalar
            def _(act):
                act.wait_ge(route, 2)
                act.activation(prob[:], logits[:], ACT.Exp).then_inc(exped, 1)
                act.wait_ge(comb_turned, 1)
                act.activation(combT[:], ps[:, 6, 0:P], ACT.Copy).then_inc(comb_out, 1)
                with act.Fori(0, NB) as blk:
                    for k in range(N3):
                        n = parts[k % 3][1]
                        wait_step(act, g_full, blk, k + 1)
                        wait_step(act, h_out, blk, max(0, k - 1))
                        act.activation(gated[0:n, k % 2, :], ps[0:n, k % 2, :], ACT.Silu).then_inc(g_out.sem, 1)
                    wait_step(act, y_full, blk, U)
                    wait_step(act, t_full, blk, 0)
                    act.activation(yT[:], ps[:, 6, :], ACT.Copy).then_inc(y_out.sem, 1)

            @block.tensor
            def _(pe):
                pe.wait_ge(loaded, LOADED)
                for t in range(NT):
                    last = pe.matmul(ps[:, 0, t * E:(t + 1) * E], xT[:, t * P:(t + 1) * P], w_r[:], start=True, stop=True)
                last.then_inc(logit_full, 1)
                pe.wait_ge(route, 24)
                pe.transpose(ps[:, 6, 0:P], comb[:].rearrange("p t e -> p (t e)"), const["ident"][:]).then_inc(comb_turned, 1)
                pe.wait_ge(comb_out, 1)

                def down(blk, u):
                    wait_step(pe, h_out, blk, 3 * u + 3)
                    if u == 0:
                        wait_step(pe, y_out, blk, 0)
                    for i, (c0, n) in enumerate(parts):
                        last = pe.matmul(ps[:, 6, :], w_d[0:n, u, i, :], hid[0:n, u % 2, i, :], start=(u == 0 and i == 0),
                                         stop=(u == U - 1 and i == 2))
                    last.then_inc(y_full.sem, 1)

                with pe.Fori(0, NB) as blk:
                    tokens = bass.ds(blk * BANK, BANK)
                    for u in range(U):
                        if u < E:
                            wait_step(pe, weighted, blk, u + 1)
                        for i, (c0, n) in enumerate(parts):
                            k = 3 * u + i
                            wait_step(pe, h_out, blk, max(0, k - 1))
                            pe.matmul(ps[0:n, k % 2, :], w_g[:, u, c0:c0 + n], xT[:, tokens], start=True, stop=True).then_inc(
                                g_full.sem, 1)
                            up_in = xw[:, u % 2, :] if u < E else xT[:, tokens]
                            pe.matmul(ps[0:n, 2 + k % 2, :], w_u[:, u, c0:c0 + n], up_in, start=True, stop=True).then_inc(
                                u_full.sem, 1)
                        if u >= 1:
                            down(blk, u - 1)
                    down(blk, U - 1)
                    wait_step(pe, y_out, blk, 1)
                    wait_step(pe, x_done, blk, 0)
                    for t in range(TB):
                        last = pe.transpose(ps[:, 7, t * P:(t + 1) * P], yT[:, t * P:(t + 1) * P], const["ident"][:])
                    last.then_inc(t_full.sem, 1)
        sem.clear()


def ffn_capacity_experts(nc, x_sb, const, w, cfg):
    E, HID = 16, 512
    CAP = int(1.25 * NT * P / E)
    HC = HID // P
    PLACES = E * CAP
    HALF = CAP // 2
    PT = PLACES // P
    with ExitStack() as ctx:
        sb = lambda n, s, d=F32: ctx.enter_context(nc.sbuf_tensor(cfg["name"] + n, s, d))
        sem = Semaphores(nc, ctx, cfg["name"])
        xn = sb("xn", [P, NT, P])
        xT = sb("xT", [P, NT * P])
        normalize_all(nc, x_sb, xn, xT, const, cfg["name"] + "ln_")
        w_r = sb("w_r", [P, E])
        w_1 = sb("w_1", [P, 2, HID])
        w_2 = sb("w_2", [P, 2, HC, P])
        small = sb("small", [P, 6, NT])
        logits = sb("logits", [P, NT, E])
        prob = sb("prob", [P, NT, E])
        hot = sb("hot", [P, NT, E])
        hot_bf = sb("hot_bf", [P, NT, E], BF16)
        place = sb("place", [P, NT, E])
        place_u = sb("place_u", [P, NT], U32)
        zeros = sb("zeros", [P, PT, P])
        slots = sb("slots", [P, PT, P])
        slotsT = sb("slotsT", [P, PLACES])
        hT = sb("hT", [P, 2, HC, CAP])
        y = sb("y", [HALF, 2, 2, P])
        back = sb("back", [P, NT, P])
        slot_dram = nc.dram_tensor(cfg["name"] + "slot_dram", (PLACES, P), F32, kind="Internal").ap()
        y_dram = nc.dram_tensor(cfg["name"] + "y_dram", (PLACES, P), F32, kind="Internal").ap()
        ps = ctx.enter_context(nc.psum_tensor(cfg["name"] + "ps", [P, 8, BANK], F32))
        loaded, logit_full, route, exped = sem("loaded"), sem("logit_full"), sem("route"), sem("exped")
        place_full, zeroed, cleared = sem("place_full"), sem("zeroed"), sem("cleared")
        slots_turned, slots_out = sem("slots_turned"), sem("slots_out")
        scattered, slots_in, gathered = (cfg["pool_dma"](n) for n in ("L0f_scattered", "L0f_slots_in", "L0f_gathered"))
        w1_in = [sem.step("w1_in0", 16), sem.step("w1_in1", 16)]
        w2_in = [sem.step("w2_in0", 16), sem.step("w2_in1", 16)]
        y_stored = [sem.step("y_stored0", 16), sem.step("y_stored1", 16)]
        h_full, h_out = sem.step("h_full", 2), sem.step("h_out", 2)
        y_full, y_out = sem.step("y_full", 1), sem.step("y_out", 1)
        x_done = sem("x_done")
        with nc.Block() as block:

            @block.sync
            def _(sp):
                sem.start(sp)
                sp.dma_start(w_r[:], w["w_r"]).then_inc(loaded, 16)
                sp.wait_ge(zeroed, 1)
                sp.dma_start(slot_dram.rearrange("(t p) d -> p t d", p=P), zeros[:]).then_inc(cleared, 16)
                with sp.Fori(0, E // 2) as pair:
                    for j in range(2):
                        e = 2 * pair + j
                        wait_step(sp, y_full, 2 * pair, 0)
                        sp.dma_start(w_1[:, j:j + 1, :], w["w_1"][bass.ds(e, 1)].rearrange("a p h -> p a h")).then_inc(
                            w1_in[j].sem, 16)
                        sp.dma_start(w_2[:, j:j + 1], w["w_2"][bass.ds(e, 1)].rearrange("a p c d -> p a c d")).then_inc(
                            w2_in[j].sem, 16)

            @block.gpsimd
            def _(pool):
                pool.memset(zeros[:], 0.0).then_inc(zeroed, 1)
                pool.memset(back[:], 0.0).then_inc(zeroed, 1)
                pool.wait_ge(cleared, 16)
                pool.wait_ge(route, 19)
                for t in range(NT):
                    pool.indirect_dma_start(slot_dram, bass.IndirectOffsetOnAxis(ap=place_u[:, t:t + 1], axis=0), xn[:, t, :],
                                            None, bounds_check=PLACES - 1, oob_is_err=False).then_inc(scattered, 16)
                pool.wait_ge(scattered, 16 * NT)
                pool.dma_start(slots[:], slot_dram.rearrange("(t p) d -> p t d", p=P)).then_inc(slots_in, 16)
                for j in range(2):
                    wait_step(pool, y_stored[j], E // 2, 0)
                pool.wait_ge(zeroed, 2)
                for t in range(NT):
                    pool.indirect_dma_start(back[:, t, :], None, y_dram,
                                            bass.IndirectOffsetOnAxis(ap=place_u[:, t:t + 1], axis=0),
                                            bounds_check=PLACES - 1, oob_is_err=False).then_inc(gathered, 16)

            @block.vector
            def _(dve):
                link = [0]

                def chain(ins):
                    link[0] += 1
                    ins.then_inc(route, 1)
                    dve.wait_ge(route, link[0])

                def spread(a):
                    return a.rearrange("p (t a) -> p t a", a=1).broadcast_to([P, NT, E])

                def by_expert(a):
                    return a.rearrange("p (a e) -> p a e", a=1).broadcast_to([P, NT, E])

                dve.wait_ge(logit_full, 1)
                lg = ps[:, 0, 0:NT * E].rearrange("p (t e) -> p t e", t=NT)
                chain(dve.tensor_reduce(small[:, 0], lg, AX, ALU.max))
                chain(dve.tensor_tensor(logits[:], lg, spread(small[:, 0]), ALU.subtract))
                dve.wait_ge(exped, 1)
                chain(dve.tensor_reduce(small[:, 1], prob[:], AX, ALU.add))
                chain(dve.reciprocal(small[:, 1], small[:, 1]))
                chain(dve.tensor_tensor(prob[:], prob[:], spread(small[:, 1]), ALU.mult))
                chain(dve.tensor_reduce(small[:, 1], prob[:], AX, ALU.max))
                chain(dve.tensor_tensor(hot[:], prob[:], spread(small[:, 1]), ALU.is_equal))
                chain(dve.tensor_tensor(hot[:], hot[:], by_expert(const["rank_down"][:, 0:E]), ALU.mult))
                chain(dve.tensor_reduce(small[:, 2], hot[:], AX, ALU.max))
                chain(dve.tensor_tensor(hot[:], hot[:], spread(small[:, 2]), ALU.is_equal))
                chain(dve.tensor_copy(hot_bf[:], hot[:]))
                dve.wait_ge(place_full, 1)
                pl = ps[:, 1, 0:NT * E].rearrange("p (t e) -> p t e", t=NT)
                chain(dve.tensor_tensor(place[:], pl, hot[:], ALU.mult))
                chain(dve.tensor_reduce(small[:, 3], place[:], AX, ALU.add))
                chain(dve.tensor_tensor(place[:], hot[:], by_expert(const["first_place"][:, 0:E]), ALU.mult))
                chain(dve.tensor_reduce(small[:, 4], place[:], AX, ALU.add))
                chain(dve.tensor_scalar(small[:, 5], small[:, 3], float(CAP), 1e6, ALU.is_ge, ALU.mult))
                chain(dve.tensor_tensor(small[:, 4], small[:, 4], small[:, 3], ALU.add))
                chain(dve.tensor_tensor(small[:, 4], small[:, 4], small[:, 5], ALU.add))
                chain(dve.tensor_copy(place_u[:], small[:, 4]))
                assert link[0] == 19
                for t in range(NT):
                    dve.wait_ge(gathered, 16 * NT)
                    dve.scalar_tensor_tensor(x_sb[:, t, :], back[:, t, :], small[:, 1, t:t + 1], x_sb[:, t, :], ALU.mult,
                                             ALU.add).then_inc(x_done, 1)

            @block.scalar
            def _(act):
                act.wait_ge(route, 2)
                act.activation(prob[:], logits[:], ACT.Exp).then_inc(exped, 1)
                for c in range(PT // 4):
                    act.wait_ge(slots_turned, 4 * (c + 1))
                    act.activation(slotsT[:, c * BANK:(c + 1) * BANK], ps[:, 2 + c % 2, :], ACT.Copy).then_inc(slots_out, 1)
                with act.Fori(0, E // 2) as pair:
                    for j in range(2):
                        e = 2 * pair + j
                        wait_step(act, y_full, 2 * pair, 0)
                        for k in range(2):
                            wait_step(act, h_full, e, k + 1)
                            act.activation(hT[:, j, 2 * k:2 * k + 2, :],
                                           ps[:, 4 + k, 0:2 * CAP].rearrange("p (c r) -> p c r", c=2), ACT.Relu).then_inc(
                                               h_out.sem, 1)
                        wait_step(act, y_full, e, 1)
                        wait_step(act, y_stored[j], pair, 0)
                        act.activation(y[:, j], ps[0:HALF, 6 + j, 0:2 * P].rearrange("p (a d) -> p a d", a=2), ACT.Copy).then_inc(
                            y_out.sem, 1)
                        wait_step(act, y_out, e, 1)
                        act.dma_start(y_dram[bass.ds(e * CAP, CAP)].rearrange("(a p) d -> p a d", p=HALF), y[:, j]).then_inc(
                            y_stored[j].sem, 16)
                for j in range(2):
                    wait_step(act, y_stored[j], E // 2, 0)

            @block.tensor
            def _(pe):
                pe.wait_ge(loaded, 16)
                for t in range(NT):
                    last = pe.matmul(ps[:, 0, t * E:(t + 1) * E], xT[:, t * P:(t + 1) * P], w_r[:], start=True, stop=True)
                last.then_inc(logit_full, 1)
                pe.wait_ge(route, 11)
                flags = hot_bf[:].rearrange("p t e -> p (t e)")
                last = pe.matmul(ps[:, 1, 0:NT * E], const["before"][:], flags, start=True, stop=True)
                for t in range(NT - 1):
                    last = pe.matmul(ps[:, 1, (t + 1) * E:NT * E].rearrange("p (t e) -> p t e", e=E), const["ones_bf"][:],
                                     hot_bf[:, t:t + 1, :].broadcast_to([P, NT - 1 - t, E]), start=False, stop=True,
                                     skip_group_check=True)
                last.then_inc(place_full, 1)
                pe.wait_ge(slots_in, 16)
                for t in range(PT):
                    if t >= 8:
                        pe.wait_ge(slots_out, t // 4 - 1)
                    pe.transpose(ps[:, 2 + t // 4 % 2, (t % 4) * P:(t % 4 + 1) * P], slots[:, t, :],
                                 const["ident"][:]).then_inc(slots_turned, 1)
                pe.wait_ge(slots_out, PT // 4)
                with pe.Fori(0, E // 2) as pair:
                    for j in range(2):
                        e = 2 * pair + j
                        rows = bass.ds(e * CAP, CAP)
                        wait_step(pe, w1_in[j], pair, 16)
                        for k in range(2):
                            wait_step(pe, h_out, e, 0)
                            for c in (2 * k, 2 * k + 1):
                                last = pe.matmul(ps[:, 4 + k, (c % 2) * CAP:(c % 2 + 1) * CAP], w_1[:, j, c * P:(c + 1) * P],
                                                 slotsT[:, rows], start=True, stop=True)
                            last.then_inc(h_full.sem, 1)
                        wait_step(pe, w2_in[j], pair, 16)
                        wait_step(pe, h_out, e, 2)
                        wait_step(pe, y_out, 2 * pair, 0)
                        for a in range(2):
                            for c in range(HC):
                                last = pe.matmul(ps[0:HALF, 6 + j, a * P:(a + 1) * P], hT[:, j, c, a * HALF:(a + 1) * HALF],
                                                 w_2[:, j, c, :], start=(c == 0), stop=(c == HC - 1))
                        last.then_inc(y_full.sem, 1)
        sem.clear()


def ffn_choosing_experts(nc, x_sb, const, w, cfg):
    E, HID, CAP, ROUNDS = 16, 512, int(S * 2.0 / 16), 6
    HC = HID // P
    BQ = P // CAP
    J = B // BQ
    ROWS = J * P
    with ExitStack() as ctx:
        sb = lambda n, s, d=F32: ctx.enter_context(nc.sbuf_tensor(cfg["name"] + n, s, d))
        sem = Semaphores(nc, ctx, cfg["name"])
        xn = sb("xn", [P, NT, P])
        xT = sb("xT", [P, NT * P])
        xn_dram = nc.dram_tensor(cfg["name"] + "xn_dram", (NT * P, P), F32, kind="Internal").ap()
        sum_dram = nc.dram_tensor(cfg["name"] + "sum_dram", (NT * P, P), F32, kind="Internal").ap()
        normalize_all(nc, x_sb, xn, xT, const, cfg["name"] + "ln_", [("xn", xn_dram), ("x", sum_dram)])
        w_r = sb("w_r", [P, E])
        temp = sb("temp", [P, 3])
        w_1 = sb("w_1", [P, 2, HID])
        b_1 = sb("b_1", [P, 2, HC])
        w_2 = sb("w_2", [P, 2, HC, P])
        b_2 = sb("b_2", [1, 2, P])
        by_token = sb("by_token", [P, QT * B, E])
        lowered = sb("lowered", [P, QT * B, E])
        exps = sb("exps", [P, QT * B, E])
        tok_small = sb("tok_small", [P, 3, QT * B])
        by_pair = sb("by_pair", [P, S])
        pair_exps = sb("pair_exps", [P, S])
        pair_small = sb("pair_small", [P, 4])
        aff = sb("aff", [P, 2, S])
        gates = sb("gates", [P, CAP])
        picks = sb("picks", [P, CAP], U32)
        picks_f = sb("picks_f", [P, 2, CAP])
        gate_col = sb("gate_col", [P, J, E])
        pick_col = sb("pick_col", [P, J, E], U32)
        rows = sb("rows", [P, E * J, P])
        rowsT = sb("rowsT", [P, E * ROWS])
        hT = sb("hT", [P, 2, HC, ROWS])
        y = sb("y", [P, 2, J, P])
        ps = ctx.enter_context(nc.psum_tensor(cfg["name"] + "ps", [P, 8, BANK], F32))
        loaded, temp_in, start, logit_full = sem("loaded"), sem("temp_in"), sem("start"), sem("logit_full")
        tok_dve, tok_act = sem.step("tok_dve", 5), sem.step("tok_act", 2)
        to_pair, to_token = sem.step("to_pair", 1), sem.step("to_token", 1)
        pair_dve, pair_act = sem.step("pair_dve", 3), sem.step("pair_act", 2)
        aff_done, top, picked, cols = sem("aff_done"), sem("top"), sem("picked"), sem("cols")
        rows_turned, rows_out = sem("rows_turned"), sem("rows_out")
        gathered, scattered = (cfg["pool_dma"](n) for n in ("L1f_gathered", "L1f_scattered"))
        w_in = [sem.step("w_in0", 64), sem.step("w_in1", 64)]
        h_full, h_out = sem.step("h_full", 2), sem.step("h_out", 2)
        y_full, y_out = sem.step("y_full", 1), sem.step("y_out", 1)
        x_back, rows_added = sem("x_back"), sem.step("rows_added", 2)

        with nc.Block() as block:

            @block.sync
            def _(sp):
                sem.start(sp)
                sp.dma_start(w_r[:], w["w_r"]).then_inc(loaded, 16)
                sp.dma_start(temp[:, 0:1], w["log_temp"].broadcast_to([P, 1])).then_inc(temp_in, 16)
                with sp.Fori(0, E // 2) as pair:
                    for j in range(2):
                        e = bass.ds(2 * pair + j, 1)
                        wait_step(sp, y_full, 2 * pair, 0)
                        sp.dma_start(w_1[:, j:j + 1, :], w["w_1"][e].rearrange("a p h -> p a h")).then_inc(w_in[j].sem, 16)
                        sp.dma_start(w_2[:, j:j + 1], w["w_2"][e].rearrange("a p c d -> p a c d")).then_inc(w_in[j].sem, 16)
                        sp.dma_start(b_1[:, j:j + 1, :], w["b_1"][e].rearrange("a p c -> p a c")).then_inc(w_in[j].sem, 16)
                        sp.dma_start(b_2[:, j, :], w["b_2"][e]).then_inc(w_in[j].sem, 16)
                sp.wait_ge(scattered, 16 * E * J)
                sp.dma_start(x_sb[:], sum_dram.rearrange("(t p) d -> p t d", p=P)).then_inc(x_back, 16)
                sp.wait_ge(x_back, 16)

            @block.gpsimd
            def _(pool):
                pool.wait_ge(cols, 4 * 2)
                for e in range(E):
                    for j in range(J):
                        pool.indirect_dma_start(rows[:, e * J + j, :], None, xn_dram,
                                                bass.IndirectOffsetOnAxis(ap=pick_col[:, j, e:e + 1], axis=0)).then_inc(
                                                    gathered, 16)
                for e in range(E):
                    if e:
                        pool.wait_ge(scattered, 16 * J * e)
                        pool.sem_inc(rows_added.sem, 1)
                    wait_step(pool, y_out, e, 1)
                    for j in range(J):
                        pool.indirect_dma_start(sum_dram, bass.IndirectOffsetOnAxis(ap=pick_col[:, j, e:e + 1], axis=0),
                                                y[:, e % 2, j, :], None, compute_op=ALU.add).then_inc(scattered, 16)

            @block.vector
            def _(dve):
                def spread(a):
                    return a.rearrange("p (t a) -> p t a", a=1).broadcast_to([P, QT * B, E])

                dve.wait_ge(start, 1)
                dve.reciprocal(temp[:, 2:3], temp[:, 1:2]).then_inc(start, 1)
                dve.wait_ge(start, 2)
                dve.wait_ge(logit_full, 1)
                for q in range(QT):
                    dve.tensor_scalar(by_token[:, q * B:(q + 1) * B, :],
                                      ps[:, 0, 0:NT * E].rearrange("p (b q e) -> p q b e", b=B, q=QT)[:, q], temp[:, 2:3],
                                      None, ALU.mult).then_inc(start, 1)
                dve.wait_ge(start, 2 + QT)
                with dve.Fori(0, ROUNDS) as r:
                    dve.tensor_reduce(tok_small[:, 0], by_token[:], AX, ALU.max).then_inc(tok_dve.sem, 1)
                    wait_step(dve, tok_dve, r, 1)
                    dve.tensor_tensor(lowered[:], by_token[:], spread(tok_small[:, 0]), ALU.subtract).then_inc(tok_dve.sem, 1)
                    wait_step(dve, tok_act, r, 1)
                    dve.tensor_reduce(tok_small[:, 1], exps[:], AX, ALU.add).then_inc(tok_dve.sem, 1)
                    wait_step(dve, tok_act, r, 2)
                    dve.tensor_tensor(by_token[:], lowered[:], spread(tok_small[:, 2]), ALU.subtract).then_inc(tok_dve.sem, 1)
                    wait_step(dve, to_pair, r, 1)
                    dve.tensor_reduce(pair_small[:, 0:1], ps[:, 1, 0:S], AX, ALU.max).then_inc(pair_dve.sem, 1)
                    wait_step(dve, pair_dve, r, 1)
                    dve.tensor_scalar(pair_small[:, 1:2], pair_small[:, 0:1], -1.0, None, ALU.mult).then_inc(pair_dve.sem, 1)
                    wait_step(dve, pair_act, r, 2)
                    dve.tensor_scalar(by_pair[:], ps[:, 1, 0:S], pair_small[:, 0:1], pair_small[:, 3:4], ALU.subtract,
                                      ALU.subtract).then_inc(pair_dve.sem, 1)
                    wait_step(dve, to_token, r, 1)
                    dve.tensor_copy(by_token[:].rearrange("p t e -> p (t e)"), ps[:, 2, 0:S]).then_inc(tok_dve.sem, 1)
                    wait_step(dve, tok_dve, r, 5)
                dve.wait_ge(aff_done, 1)
                n = 0
                for k in range(CAP // 8):
                    a, eight = aff[:, k % 2, :], slice(8 * k, 8 * k + 8)
                    dve.max(gates[:, eight], a).then_inc(top, 1)
                    n += 1
                    dve.wait_ge(top, n)
                    dve.max_index(picks[:, eight], gates[:, eight], a).then_inc(top, 1)
                    dve.match_replace(aff[:, 1 - k % 2, :], gates[:, eight], a, -1.0).then_inc(top, 1)
                    n += 2
                    dve.wait_ge(top, n)
                dve.tensor_copy(picks_f[:, 0, :], picks[:]).then_inc(top, 1)
                dve.wait_ge(top, n + 1)
                dve.tensor_scalar(picks_f[:, 1, :], picks_f[:, 0, :], const["first_token"][:, 0:1], None, ALU.add).then_inc(top, 1)
                dve.wait_ge(picked, 1)
                for i, dst in enumerate((pick_col, gate_col)):
                    for q in range(BQ):
                        dve.tensor_copy(dst[CAP * q:CAP * (q + 1)],
                                        ps[0:CAP, 3, i * P:(i + 1) * P].rearrange("c (j q e) -> c q j e", j=J, q=BQ)[:, q]).then_inc(
                                            cols, 1)
                dve.wait_ge(cols, 2 * BQ)
                with dve.Fori(0, E // 2) as pair:
                    for s in range(2):
                        e = 2 * pair + s
                        wait_step(dve, rows_added, pair, 0)
                        wait_step(dve, y_full, e, 1)
                        for j in range(J):
                            last = dve.tensor_scalar(y[:, s, j, :], ps[:, 6 + s, j * P:(j + 1) * P], gate_col[:, j, bass.ds(e, 1)],
                                                     None, ALU.mult)
                        last.then_inc(y_out.sem, 1)

            @block.scalar
            def _(act):
                act.wait_ge(temp_in, 16)
                act.activation(temp[:, 1:2], temp[:, 0:1], ACT.Exp).then_inc(start, 1)
                with act.Fori(0, ROUNDS) as r:
                    wait_step(act, tok_dve, r, 2)
                    act.activation(exps[:], lowered[:], ACT.Exp).then_inc(tok_act.sem, 1)
                    wait_step(act, tok_dve, r, 3)
                    act.activation(tok_small[:, 2], tok_small[:, 1], ACT.Ln).then_inc(tok_act.sem, 1)
                    wait_step(act, pair_dve, r, 2)
                    act.activation(pair_exps[:], ps[:, 1, 0:S], ACT.Exp, bias=pair_small[:, 1:2],
                                   accum_out=pair_small[:, 2:3]).then_inc(pair_act.sem, 1)
                    wait_step(act, pair_act, r, 1)
                    act.activation(pair_small[:, 3:4], pair_small[:, 2:3], ACT.Ln).then_inc(pair_act.sem, 1)
                wait_step(act, pair_dve, ROUNDS, 0)
                act.activation(aff[:, 0, :], by_pair[:], ACT.Exp).then_inc(aff_done, 1)
                for c in range(E * J // 4):
                    act.wait_ge(rows_turned, 4 * (c + 1))
                    act.activation(rowsT[:, c * BANK:(c + 1) * BANK], ps[:, 1 + c % 2, :], ACT.Copy).then_inc(rows_out, 1)
                with act.Fori(0, E // 2) as pair:
                    for s in range(2):
                        e = 2 * pair + s
                        wait_step(act, w_in[s], pair, 64)
                        wait_step(act, y_full, 2 * pair, 0)
                        for k in range(2):
                            wait_step(act, h_full, e, k + 1)
                            for c in (2 * k, 2 * k + 1):
                                last = act.activation(hT[:, s, c, :], ps[:, 4 + k, (c % 2) * ROWS:(c % 2 + 1) * ROWS],
                                                      ACT.Gelu_apprx_tanh, bias=b_1[:, s, c:c + 1])
                            last.then_inc(h_out.sem, 1)

            @block.tensor
            def _(pe):
                pe.wait_ge(loaded, 16)
                for t in range(NT):
                    last = pe.matmul(ps[:, 0, t * E:(t + 1) * E], xT[:, t * P:(t + 1) * P], w_r[:], start=True, stop=True)
                last.then_inc(logit_full, 1)
                with pe.Fori(0, ROUNDS) as r:
                    wait_step(pe, tok_dve, r, 4)
                    for q in range(QT):
                        last = pe.transpose(ps[:, 1, q * P:(q + 1) * P],
                                            by_token[:, q * B:(q + 1) * B, :].rearrange("p b e -> p (b e)"), const["ident"][:])
                    last.then_inc(to_pair.sem, 1)
                    wait_step(pe, pair_dve, r, 3)
                    for q in range(QT):
                        last = pe.transpose(ps[:, 2, q * P:(q + 1) * P], by_pair[:, q * P:(q + 1) * P], const["ident"][:])
                    last.then_inc(to_token.sem, 1)
                pe.wait_ge(top, 3 * (CAP // 8) + 2)
                pe.transpose(ps[0:CAP, 3, 0:P], picks_f[:, 1, :], const["ident"][:])
                pe.transpose(ps[0:CAP, 3, P:2 * P], gates[:], const["ident"][:]).then_inc(picked, 1)
                for t in range(E * J):
                    pe.wait_ge(gathered, 16 * E * J)
                    if t >= 8:
                        pe.wait_ge(rows_out, t // 4 - 1)
                    pe.transpose(ps[:, 1 + t // 4 % 2, (t % 4) * P:(t % 4 + 1) * P], rows[:, t, :],
                                 const["ident"][:]).then_inc(rows_turned, 1)
                pe.wait_ge(rows_out, E * J // 4)
                with pe.Fori(0, E // 2) as pair:
                    for s in range(2):
                        e = 2 * pair + s
                        wait_step(pe, w_in[s], pair, 64)
                        for k in range(2):
                            wait_step(pe, h_out, e, 0)
                            for c in (2 * k, 2 * k + 1):
                                last = pe.matmul(ps[:, 4 + k, (c % 2) * ROWS:(c % 2 + 1) * ROWS], w_1[:, s, c * P:(c + 1) * P],
                                                 rowsT[:, bass.ds(e * ROWS, ROWS)], start=True, stop=True)
                            last.then_inc(h_full.sem, 1)
                        wait_step(pe, h_out, e, 2)
                        wait_step(pe, y_out, 2 * pair, 0)
                        for j in range(J):
                            out = ps[:, 6 + s, j * P:(j + 1) * P]
                            for c in range(HC):
                                pe.matmul(out, hT[:, s, c, j * P:(j + 1) * P], w_2[:, s, c, :], start=(c == 0), stop=False)
                            last = pe.matmul(out, const["ones"][0:1, :], b_2[:, s, :], start=False, stop=True)
                        last.then_inc(y_full.sem, 1)
        sem.clear()




def attention_fidelity(nc, x_sb, y_all, const, w, name):
    H, HD, NQ = 8, 16, 8
    ratio, eps_cos = 0.5, 1e-8
    QROWS = H * NQ
    with ExitStack() as ctx:
        sb = lambda n, s, d=F32: ctx.enter_context(nc.sbuf_tensor(name + n, s, d))
        sem = Semaphores(nc, ctx, name)
        w_q, w_k, w_v = sb("w_q", [P, P]), sb("w_k", [P, P]), sb("w_v", [P, P])
        b_q, b_k, b_v = sb("b_q", [P, 1]), sb("b_k", [P, 1]), sb("b_v", [P, P])
        w_c = sb("w_c", [P, QROWS])
        b_c = sb("b_c", [QROWS, 1])
        b_cr = sb("b_cr", [P, QROWS])
        w_o, b_o = sb("w_o", [P, 2, P]), sb("b_o", [P, P])
        stats, mean_var = sb("stats", [P, QT, 6]), sb("mean_var", [P, QT, 2])
        rstd, fill = sb("rstd", [P, QT]), sb("fill", [P, 1])
        xn, xT = sb("xn", [P, QT, P]), sb("xT", [P, S])
        qT, kT = sb("qT", [P, S]), sb("kT", [P, S])
        cqT, ckT = sb("cqT", [P, S]), sb("ckT", [P, S])
        qm, cqm = sb("qm", [P, H, S]), sb("cqm", [P, H, S])
        v = sb("v", [P, QT, H, 32])
        c_tok = sb("c_tok", [P, 2 * QT, QROWS])
        c_sq = sb("c_sq", [P, 2 * QT, QROWS])
        norm2, rnorm = sb("norm2", [P, 2 * QT, H]), sb("rnorm", [P, 2 * QT, H])
        rkT = sb("rkT", [P, P])
        inv = sb("inv", [P, 2, QT, S])
        fid, fidc, sine = sb("fid", [P, 2, QT, S]), sb("fidc", [P, 2, QT, S]), sb("sine", [P, 2, QT, S])
        mixed = sb("mixed", [P, 2, QT, S])
        z = sb("z", [P, H, QT, S])
        mx, negm = sb("mx", [P, H, QT]), sb("negm", [P, H, QT])
        prob = sb("prob", [P, 2, QT, S])
        probT = sb("probT", [P, H, QT, S])
        sums, oT = sb("sums", [P, 2, S]), sb("oT", [P, 2, S])
        attn = sb("attn", [P, QT, P])
        ps = ctx.enter_context(nc.psum_tensor(name + "ps", [P, 8, BANK], F32))

        loaded, ready = sem("loaded"), sem("ready")
        ln_done, ln_pool = sem.step("ln_done", 3 * QT + 1), sem.step("ln_pool", 1)
        made = sem.step("made", 6)
        copied = sem.step("copied", 6)
        v_out, c_steps, normed = sem.step("v_out", 1), sem.step("c_steps", 4), sem.step("normed", 1)
        masked = sem.step("masked", 2 * H)
        s_full, inv_done, mix_done = sem.step("s_full", H), sem.step("inv_done", H), sem.step("mix_done", H)
        fid_done, clamp_done, sin_done = sem.step("fid_done", H), sem.step("clamp_done", H), sem.step("sin_done", H)
        mx_done = sem.step("mx_done", H)
        u_done, z_done = sem.step("u_done", H), sem.step("z_done", H)
        neg_done, exp_done, p_turned = sem.step("neg_done", 1), sem.step("exp_done", H), sem.step("p_turned", H)
        p_out, o_full = sem.step("p_out", H), sem.step("o_full", 2)
        sum_steps, o_done = sem.step("sum_steps", 4), sem.step("o_done", 2)
        y_full, y_steps = sem.step("y_full", 1), sem.step("y_steps", 1 + QT)
        loads = [(w_q[:], w["w_q"]), (w_k[:], w["w_k"]), (w_v[:], w["w_v"]), (b_q[:], w["b_q"]), (b_k[:], w["b_k"]),
                 (b_v[:], w["b_v"].broadcast_to([P, P])), (w_c[:], w["w_c"]), (b_c[:], w["b_c"]),
                 (b_cr[:], w["b_cr"].broadcast_to([P, QROWS])), (w_o[:], w["w_o"]), (b_o[:], w["b_o"].broadcast_to([P, P]))]
        LOADED = 16 * len(loads)

        with nc.Block() as block:

            @block.sync
            def _(sp):
                sem.start(sp)
                for dst, s in loads:
                    sp.dma_start(dst, s).then_inc(loaded, 16)

            @block.gpsimd
            def _(pool):
                pool.memset(v[:], 1.0).then_inc(ready, 1)
                for t in (cqT, ckT, rkT):
                    pool.memset(t[:], 0.0).then_inc(ready, 1)
                pool.wait_ge(ready, 4)
                with pool.Fori(0, B) as b:
                    wait_step(pool, ln_done, b, 2 * QT + 1)
                    pool.tensor_tensor(rstd[:], mean_var[:, :, 1], const["minus_half"][:, 0:QT],
                                       ALU.pow).then_inc(ln_pool.sem, 1)
                    wait_step(pool, c_steps, b, 4)
                    pool.tensor_tensor(rnorm[:].rearrange("p a h -> p (a h)"), norm2[:].rearrange("p a h -> p (a h)"),
                                       const["minus_half"][:, 0:1].broadcast_to([P, 2 * QT * H]), ALU.pow).then_inc(normed.sem, 1)
                    wait_step(pool, copied, b, 5)
                    wait_step(pool, s_full, b, 0)
                    for h in range(H):
                        pool.tensor_tensor(cqm[:, h, :], cqT[:], const["rows_of_8"][:, h:h + 1].broadcast_to([P, S]),
                                           ALU.mult).then_inc(masked.sem, 1)
                        pool.tensor_tensor(qm[:, h, :], qT[:], const["rows_of_16"][:, h:h + 1].broadcast_to([P, S]),
                                           ALU.mult).then_inc(masked.sem, 1)

            @block.vector
            def _(dve):
                dve.wait_ge(ready, 4)
                dve.wait_ge(loaded, LOADED)
                with dve.Fori(0, B) as b:
                    for t in range(QT):
                        dve.bn_stats(stats[:, t, :], x_sb[:, bass.ds(b * QT + t, 1), :]).then_inc(ln_done.sem, 1)
                    wait_step(dve, ln_done, b, QT)
                    dve.memset(fill[:], 0.0)
                    for t in range(QT):
                        dve.bn_aggr(mean_var[:, t, :], stats[:, t, :]).then_inc(ln_done.sem, 1)
                    wait_step(dve, ln_done, b, 2 * QT)
                    dve.tensor_scalar(mean_var[:, :, 1], mean_var[:, :, 1], EPS, None, ALU.add).then_inc(ln_done.sem, 1)
                    wait_step(dve, ln_pool, b, 1)
                    for t in range(QT):
                        dve.tensor_scalar(xn[:, t, :], x_sb[:, bass.ds(b * QT + t, 1), :], mean_var[:, t, 0:1],
                                          rstd[:, t:t + 1], ALU.subtract, ALU.mult).then_inc(ln_done.sem, 1)
                    wait_step(dve, made, b, 3)
                    for t in range(QT):
                        last = dve.tensor_tensor(v[:, t, :, 0:HD], ps[:, 2, t * P:(t + 1) * P].rearrange("p (h d) -> p h d", h=H),
                                                 b_v[:].rearrange("p (h d) -> p h d", h=H), ALU.add)
                    last.then_inc(v_out.sem, 1)
                    wait_step(dve, made, b, 5)
                    dve.tensor_tensor(c_tok[:], ps[:, 4, 0:2 * QT * QROWS].rearrange("p (a c) -> p a c", c=QROWS),
                                      b_cr[:].rearrange("p (a c) -> p a c", a=1).broadcast_to([P, 2 * QT, QROWS]),
                                      ALU.add).then_inc(c_steps.sem, 1)
                    wait_step(dve, c_steps, b, 1)
                    dve.tensor_tensor(c_sq[:], c_tok[:], c_tok[:], ALU.mult).then_inc(c_steps.sem, 1)
                    wait_step(dve, c_steps, b, 2)
                    dve.tensor_reduce(norm2[:].rearrange("p a h -> p (a h)"),
                                      c_sq[:].rearrange("p a (h c) -> p (a h) c", c=NQ), AX, ALU.add).then_inc(c_steps.sem, 1)
                    wait_step(dve, c_steps, b, 3)
                    dve.tensor_scalar(norm2[:], norm2[:], 1e-37, None, ALU.max).then_inc(c_steps.sem, 1)
                    wait_step(dve, normed, b, 1)

                    def similarity(h):
                        wait_step(dve, s_full, b, h + 1)
                        s = h % 2
                        for t in range(QT):
                            last = dve.tensor_scalar(inv[:, s, t, :], ps[:, 5 + s, 0:S], rnorm[:, t, h:h + 1], 1.0 / eps_cos,
                                                     ALU.mult, ALU.min)
                        last.then_inc(inv_done.sem, 1)
                        wait_step(dve, inv_done, b, h + 1)
                        dve.tensor_tensor(fid[:, s], ps[:, 1 + s, :].rearrange("p (t k) -> p t k", t=QT), inv[:, s],
                                          ALU.mult).then_inc(fid_done.sem, 1)
                        wait_step(dve, fid_done, b, h + 1)
                        wait_step(dve, sin_done, b, max(0, h - 1))
                        dve.tensor_scalar(fidc[:, s], fid[:, s], 1.0 - 2.0 ** -22, 2.0 ** -22 - 1.0, ALU.min,
                                          ALU.max).then_inc(clamp_done.sem, 1)
                        dve.scalar_tensor_tensor(mixed[:, s].rearrange("p t k -> p (t k)"), ps[:, 3 + s, :], HD ** -0.5,
                                                 fid[:, s].rearrange("p t k -> p (t k)"), ALU.mult, ALU.add).then_inc(
                                                     mix_done.sem, 1)

                    def weights(h):
                        s = h % 2
                        wait_step(dve, sin_done, b, h + 1)
                        flat = lambda a: a.rearrange("p t k -> p (t k)")
                        dve.scalar_tensor_tensor(flat(fid[:, s]), flat(sine[:, s]), 0.1, flat(fid[:, s]), ALU.mult,
                                                 ALU.mult).then_inc(u_done.sem, 1)
                        wait_step(dve, u_done, b, h + 1)
                        wait_step(dve, mix_done, b, h + 1)
                        dve.tensor_tensor(z[:, h], fid[:, s], mixed[:, s], ALU.add).then_inc(z_done.sem, 1)
                        wait_step(dve, z_done, b, h + 1)
                        dve.tensor_reduce(mx[:, h, :], z[:, h], AX, ALU.max).then_inc(mx_done.sem, 1)

                    for h in range(H + 1):
                        if h < H:
                            similarity(h)
                        if h >= 1:
                            weights(h - 1)
                    wait_step(dve, mx_done, b, H)
                    dve.tensor_scalar(negm[:], mx[:], -ratio, None, ALU.mult).then_inc(neg_done.sem, 1)
                    for h in range(H):
                        wait_step(dve, p_turned, b, h + 1)
                        dve.tensor_copy(probT[:, h].rearrange("p t k -> p (t k)"), ps[:, 1 + h % 2, :]).then_inc(p_out.sem, 1)
                    for g in range(2):
                        wait_step(dve, o_full, b, g + 1)
                        dve.memset(fill[:], 0.0)
                        dve.stream_shuffle(sums[:, g, :], ps[:, 7 - g, 0:S], [HD] * 32).then_inc(sum_steps.sem, 1)
                        wait_step(dve, sum_steps, b, 2 * g + 1)
                        dve.reciprocal(sums[:, g, :], sums[:, g, :]).then_inc(sum_steps.sem, 1)
                        wait_step(dve, sum_steps, b, 2 * g + 2)
                        dve.tensor_tensor(oT[:, g, :], ps[:, 7 - g, 0:S], sums[:, g, :], ALU.mult).then_inc(o_done.sem, 1)
                    wait_step(dve, y_full, b, 1)
                    dve.tensor_tensor(attn[:], ps[:, 0, 0:S].rearrange("p (t d) -> p t d", t=QT), xn[:], ALU.add).then_inc(
                        y_steps.sem, 1)
                    wait_step(dve, y_steps, b, 1)
                    for t in range(QT):
                        dve.tensor_tensor(y_all[:, bass.ds(b * QT + t, 1), :], attn[:, t:t + 1, :],
                                          b_o[:].rearrange("p (a d) -> p a d", a=1), ALU.add).then_inc(y_steps.sem, 1)

            @block.scalar
            def _(act):
                act.wait_ge(ready, 4)
                act.wait_ge(loaded, LOADED)
                with act.Fori(0, B) as b:
                    wait_step(act, made, b, 1)
                    act.activation(xT[:], ps[:, 0, 0:S], ACT.Copy).then_inc(copied.sem, 1)
                    wait_step(act, made, b, 2)
                    act.activation(qT[:], ps[:, 1, 0:S], ACT.Identity, bias=b_q[:]).then_inc(copied.sem, 1)
                    act.activation(kT[:], ps[:, 1, S:2 * S], ACT.Identity, bias=b_k[:]).then_inc(copied.sem, 1)
                    wait_step(act, made, b, 4)
                    act.activation(cqT[0:QROWS, :], ps[0:QROWS, 3, 0:S], ACT.Identity, bias=b_c[:]).then_inc(copied.sem, 1)
                    act.activation(ckT[0:QROWS, :], ps[0:QROWS, 3, S:2 * S], ACT.Identity, bias=b_c[:]).then_inc(copied.sem, 1)
                    wait_step(act, made, b, 6)
                    act.activation(rkT[0:2 * H, :], ps[0:2 * H, 0, 0:P], ACT.Copy).then_inc(copied.sem, 1)
                    for h in range(H):
                        wait_step(act, clamp_done, b, h + 1)
                        wait_step(act, u_done, b, max(0, h - 1))
                        act.activation(sine[:, h % 2], fidc[:, h % 2], ACT.Sin, scale=float(np.pi)).then_inc(sin_done.sem, 1)
                    wait_step(act, neg_done, b, 1)
                    for h in range(H):
                        wait_step(act, p_turned, b, max(0, h - 1))
                        for t in range(QT):
                            last = act.activation(prob[:, h % 2, t, :], z[:, h, t, :], ACT.Exp, scale=ratio,
                                                  bias=negm[:, h, t:t + 1])
                        last.then_inc(exp_done.sem, 1)

            @block.tensor
            def _(pe):
                pe.wait_ge(ready, 4)
                pe.wait_ge(loaded, LOADED)
                with pe.Fori(0, B) as b:
                    wait_step(pe, ln_done, b, 3 * QT + 1)
                    wait_step(pe, y_steps, b, 0)
                    for t in range(QT):
                        last = pe.transpose(ps[:, 0, t * P:(t + 1) * P], xn[:, t, :], const["ident"][:])
                    last.then_inc(made.sem, 1)
                    wait_step(pe, copied, b, 1)
                    pe.matmul(ps[:, 1, 0:S], w_q[:], xT[:], start=True, stop=True)
                    pe.matmul(ps[:, 1, S:2 * S], w_k[:], xT[:], start=True, stop=True).then_inc(made.sem, 1)
                    for t in range(QT):
                        last = pe.matmul(ps[:, 2, t * P:(t + 1) * P], xT[:, t * P:(t + 1) * P], w_v[:], start=True, stop=True)
                    last.then_inc(made.sem, 1)
                    wait_step(pe, copied, b, 3)
                    pe.matmul(ps[0:QROWS, 3, 0:S], w_c[:], qT[:], start=True, stop=True)
                    pe.matmul(ps[0:QROWS, 3, S:2 * S], w_c[:], kT[:], start=True, stop=True).then_inc(made.sem, 1)
                    for a in range(2 * QT):
                        src = qT if a < QT else kT
                        last = pe.matmul(ps[:, 4, a * QROWS:(a + 1) * QROWS], src[:, (a % QT) * P:(a % QT + 1) * P], w_c[:],
                                         start=True, stop=True)
                    last.then_inc(made.sem, 1)
                    wait_step(pe, normed, b, 1)
                    pe.transpose(ps[0:2 * H, 0, 0:P], rnorm[:, QT:2 * QT, :].rearrange("p a h -> p (a h)"),
                                 const["ident"][:]).then_inc(made.sem, 1)
                    wait_step(pe, copied, b, 6)
                    wait_step(pe, v_out, b, 1)
                    for h in range(H):
                        s = h % 2
                        wait_step(pe, mix_done, b, max(0, h - 1))
                        wait_step(pe, masked, b, 2 * h + 2)
                        for t in range(QT):
                            pe.matmul(ps[:, 5 + s, t * P:(t + 1) * P], const["pick_row"][:, t * H + h, :], rkT[:], start=True,
                                      stop=True)
                        for t in range(QT):
                            pe.matmul(ps[:, 1 + s, t * S:(t + 1) * S], cqm[:, h, t * P:(t + 1) * P], ckT[:], start=True, stop=True)
                        for t in range(QT):
                            last = pe.matmul(ps[:, 3 + s, t * S:(t + 1) * S], qm[:, h, t * P:(t + 1) * P], kT[:], start=True,
                                             stop=True)
                        last.then_inc(s_full.sem, 1)

                    def values(g):
                        wait_step(pe, p_out, b, 4 * g + 4)
                        for t in range(QT):
                            for j in range(4):
                                last = pe.matmul(ps[32 * j:32 * j + 32, 7 - g, 0:S], v[:, t, 4 * g + j, :], probT[:, 4 * g + j, t, :],
                                                 start=(t == 0), stop=(t == QT - 1), skip_group_check=True)
                        last.then_inc(o_full.sem, 1)

                    wait_step(pe, mix_done, b, H)
                    for h in range(H):
                        wait_step(pe, exp_done, b, h + 1)
                        wait_step(pe, p_out, b, max(0, h - 1))
                        for q in range(QT):
                            for t in range(QT):
                                last = pe.transpose(ps[:, 1 + h % 2, t * S + q * P:t * S + (q + 1) * P],
                                                    prob[:, h % 2, q, t * P:(t + 1) * P], const["ident"][:])
                        last.then_inc(p_turned.sem, 1)
                        if h == 5:
                            values(0)
                    values(1)
                    wait_step(pe, o_done, b, 2)
                    for t in range(QT):
                        for g in range(2):
                            last = pe.matmul(ps[:, 0, t * P:(t + 1) * P], oT[:, g, t * P:(t + 1) * P], w_o[:, g, :],
                                             start=(g == 0), stop=(g == 1))
                    last.then_inc(y_full.sem, 1)
        sem.clear()


def fidelity_tail(nc, x_sb, y_all, const, w, name):
    FF, NQ = 512, 8
    FC, NB = FF // P, NT * P // BANK
    TB = BANK // P
    with ExitStack() as ctx:
        sb = lambda n, s, d=F32: ctx.enter_context(nc.sbuf_tensor(name + n, s, d))
        sem = Semaphores(nc, ctx, name)
        n1, n1T = sb("n1", [P, NT, P]), sb("n1T", [P, NT * P])
        normalize_all(nc, y_all, n1, n1T, const, name + "ln1_")
        x1, x1T = sb("x1", [P, NT, P]), sb("x1T", [P, NT * P])
        g1c, beta1c = sb("g1c", [P, 1]), sb("beta1c", [P, 1])
        rows = sb("rows", [P, 4, P])
        w_1, b_1 = sb("w_1", [P, FF]), sb("b_1", [P, FC])
        w_m, b_m = sb("w_m", [P, FC, NQ]), sb("b_m", [NQ, 1])
        w_qo, b_qo = sb("w_qo", [NQ, FF]), sb("b_qo", [P, FC])
        w_2, b_2 = sb("w_2", [P, FC, P]), sb("b_2", [P, 1])
        hT, haT = sb("hT", [P, FC, BANK]), sb("haT", [P, FC, BANK])
        qmT, turns, whole = sb("qmT", [NQ, BANK]), sb("turns", [NQ, BANK]), sb("whole", [NQ, BANK])
        folded, neg = sb("folded", [NQ, BANK]), sb("neg", [NQ, BANK])
        tanh, cosine, qeT = sb("tanh", [NQ, BANK]), sb("cosine", [NQ, BANK]), sb("qeT", [NQ, BANK])
        quarter = sb("quarter", [NQ, 1])
        ffT = sb("ffT", [P, BANK])
        ps = ctx.enter_context(nc.psum_tensor(name + "ps", [P, 8, BANK], F32))
        loaded, affine, x1t_done = sem("loaded"), sem("affine"), sem("x1t_done")
        h_full, h_out = sem.step("h_full", FC), sem.step("h_out", FC)
        q_full, q_out, q_steps = sem.step("q_full", 1), sem.step("q_out", 1), sem.step("q_steps", 7)
        trig, a_full, a_out = sem.step("trig", 2), sem.step("a_full", FC), sem.step("a_out", FC)
        f_full, f_out, t_full, y_done = sem.step("f_full", 1), sem.step("f_out", 1), sem.step("t_full", 1), sem.step("y_done", 1)
        loads = [(g1c[:], w["g1c"]), (beta1c[:], w["beta1c"]), (w_1[:], w["w_1"]), (b_1[:], w["b_1"]), (w_m[:], w["w_m"]),
                 (b_m[:], w["b_m"]), (w_qo[:], w["w_qo"]), (b_qo[:], w["b_qo"]), (w_2[:], w["w_2"]), (b_2[:], w["b_2"])]
        loads += [(rows[:, i, :], w["rows"][i:i + 1, :].broadcast_to([P, P])) for i in range(4)]
        LOADED = 16 * len(loads)
        ROUND = 1.5 * 2.0 ** 23

        with nc.Block() as block:

            @block.sync
            def _(sp):
                sem.start(sp)
                for dst, s in loads:
                    sp.dma_start(dst, s).then_inc(loaded, 16)

            @block.vector
            def _(dve):
                def row(i, n=NT):
                    return rows[:, i:i + 1, :].broadcast_to([P, n, P])

                dve.wait_ge(loaded, LOADED)
                dve.tensor_tensor(x1[:], n1[:], row(0), ALU.mult).then_inc(affine, 1)
                dve.wait_ge(affine, 1)
                dve.tensor_tensor(x1[:], x1[:], row(1), ALU.add).then_inc(affine, 1)
                dve.memset(quarter[:], float(np.pi / 2)).then_inc(affine, 1)
                dve.wait_ge(affine, 3)
                with dve.Fori(0, NB) as blk:
                    wait_step(dve, q_out, blk, 1)
                    dve.tensor_scalar(turns[:], qmT[:], 0.125, None, ALU.mult).then_inc(q_steps.sem, 1)
                    wait_step(dve, q_steps, blk, 1)
                    dve.tensor_scalar(whole[:], turns[:], ROUND, None, ALU.add).then_inc(q_steps.sem, 1)
                    wait_step(dve, q_steps, blk, 2)
                    dve.scalar_tensor_tensor(folded[:], whole[:], ROUND, turns[:], ALU.subtract, ALU.subtract).then_inc(
                        q_steps.sem, 1)
                    wait_step(dve, q_steps, blk, 3)
                    dve.tensor_scalar(neg[:], folded[:], -1.0, None, ALU.mult).then_inc(q_steps.sem, 1)
                    wait_step(dve, q_steps, blk, 4)
                    dve.tensor_tensor(folded[:], folded[:], neg[:], ALU.max).then_inc(q_steps.sem, 1)
                    wait_step(dve, q_steps, blk, 5)
                    dve.tensor_scalar(folded[:], folded[:], 0.5, None, ALU.min).then_inc(q_steps.sem, 1)
                    wait_step(dve, trig, blk, 2)
                    dve.tensor_tensor(qeT[:], tanh[:], cosine[:], ALU.mult).then_inc(q_steps.sem, 1)
                    wait_step(dve, t_full, blk, 1)
                    tiles = bass.ds(blk * TB, TB)
                    dve.tensor_tensor(x1[:, tiles, :], x1[:, tiles, :], ps[:, 7, :].rearrange("p (t d) -> p t d", t=TB),
                                      ALU.add).then_inc(y_done.sem, 1)

            @block.scalar
            def _(act):
                act.wait_ge(loaded, LOADED)
                for c in range(4):
                    act.activation(x1T[:, c * BANK:(c + 1) * BANK], n1T[:, c * BANK:(c + 1) * BANK], ACT.Identity,
                                   scale=g1c[:], bias=beta1c[:]).then_inc(x1t_done, 1)
                act.wait_ge(affine, 3)
                with act.Fori(0, NB) as blk:
                    for c in range(FC):
                        wait_step(act, h_full, blk, c + 1)
                        act.activation(hT[:, c, :], ps[:, c % 2, :], ACT.Identity, bias=b_1[:, c:c + 1]).then_inc(h_out.sem, 1)
                    wait_step(act, q_full, blk, 1)
                    wait_step(act, q_steps, blk, 0)
                    act.activation(qmT[:], ps[0:NQ, 2, :], ACT.Identity, bias=b_m[:]).then_inc(q_out.sem, 1)
                    wait_step(act, q_out, blk, 1)
                    act.activation(tanh[:], qmT[:], ACT.Tanh).then_inc(trig.sem, 1)
                    wait_step(act, q_steps, blk, 6)
                    act.activation(cosine[:], folded[:], ACT.Sin, scale=float(-2 * np.pi), bias=quarter[:]).then_inc(trig.sem, 1)
                    for c in range(FC):
                        wait_step(act, a_full, blk, c + 1)
                        act.activation(haT[:, c, :], ps[:, 3 + c % 2, :], ACT.Identity, bias=b_qo[:, c:c + 1]).then_inc(a_out.sem, 1)
                    wait_step(act, f_full, blk, 1)
                    wait_step(act, t_full, blk, 0)
                    act.activation(ffT[:], ps[:, 5, :], ACT.Identity, bias=b_2[:]).then_inc(f_out.sem, 1)

            @block.tensor
            def _(pe):
                pe.wait_ge(loaded, LOADED)
                pe.wait_ge(x1t_done, 4)
                with pe.Fori(0, NB) as blk:
                    for c in range(FC):
                        wait_step(pe, h_out, blk, max(0, c - 1))
                        pe.matmul(ps[:, c % 2, :], w_1[:, c * P:(c + 1) * P], x1T[:, bass.ds(blk * BANK, BANK)], start=True,
                                  stop=True).then_inc(h_full.sem, 1)
                    wait_step(pe, h_out, blk, FC)
                    for c in range(FC):
                        last = pe.matmul(ps[0:NQ, 2, :], w_m[:, c, :], hT[:, c, :], start=(c == 0), stop=(c == FC - 1))
                    last.then_inc(q_full.sem, 1)
                    wait_step(pe, q_steps, blk, 7)
                    for c in range(FC):
                        wait_step(pe, a_out, blk, max(0, c - 1))
                        pe.matmul(ps[:, 3 + c % 2, :], w_qo[:, c * P:(c + 1) * P], qeT[:], start=True, stop=True).then_inc(
                            a_full.sem, 1)
                    wait_step(pe, a_out, blk, FC)
                    for c in range(FC):
                        last = pe.matmul(ps[:, 5, :], w_2[:, c, :], haT[:, c, :], start=(c == 0), stop=(c == FC - 1))
                    last.then_inc(f_full.sem, 1)
                    wait_step(pe, f_out, blk, 1)
                    wait_step(pe, y_done, blk, 0)
                    for t in range(TB):
                        last = pe.transpose(ps[:, 7, t * P:(t + 1) * P], ffT[:, t * P:(t + 1) * P], const["ident"][:])
                    last.then_inc(t_full.sem, 1)
        sem.clear()
        normalize_all(nc, x1, n1, None, const, name + "ln2_")
        sem = Semaphores(nc, ctx, name)
        added = sem("added")
        with nc.Block() as block:

            @block.vector
            def _(dve):
                dve.tensor_tensor(n1[:], n1[:], rows[:, 2:3, :].broadcast_to([P, NT, P]), ALU.mult).then_inc(added, 1)
                dve.wait_ge(added, 1)
                dve.tensor_tensor(n1[:], n1[:], rows[:, 3:4, :].broadcast_to([P, NT, P]), ALU.add).then_inc(added, 1)
                dve.wait_ge(added, 2)
                dve.tensor_tensor(x_sb[:], x_sb[:], n1[:], ALU.add).then_inc(added, 1)
        sem.clear()


def attention_fidelity_layer(nc, x_sb, const, w, cfg):
    with nc.sbuf_tensor(cfg["name"] + "y_all", [P, NT, P], F32) as y_all:
        attention_fidelity(nc, x_sb, y_all, const, w, cfg["name"])
        fidelity_tail(nc, x_sb, y_all, const, w, cfg["name"] + "tail_")


def load_constants(nc, ctx, x_sb, x, const_in):
    const = {n: ctx.enter_context(nc.sbuf_tensor("const_" + n, list(a.shape), BF16 if n in BF16_CONSTS else F32))
             for n, a in const_in.items()}
    with ExitStack() as own:
        sem = Semaphores(nc, own, "start_")
        loaded, rounded = sem("loaded"), sem("rounded")
        wide = {n: own.enter_context(nc.sbuf_tensor("wide_" + n, list(const_in[n].shape), F32)) for n in BF16_CONSTS}
        with nc.Block() as block:

            @block.sync
            def _(sp):
                sp.dma_start(x_sb[:], x.rearrange("b (t p) d -> p (b t) d", p=P)).then_inc(loaded, 16)
                for n, a in const_in.items():
                    sp.dma_start(wide[n][:] if n in wide else const[n][:], a).then_inc(loaded, 16)

            @block.vector
            def _(dve):
                dve.wait_ge(loaded, 16 * (1 + len(const_in)))
                for n in BF16_CONSTS:
                    dve.tensor_copy(const[n][:], wide[n][:]).then_inc(rounded, 1)
        sem.clear()
    return const


def decoder(nc, x, out, const_in, layers):
    steps = {"L0f": ffn_capacity_experts, "L1f": ffn_choosing_experts, "L2f": ffn_dense_experts, "L3f": ffn_argmax_experts,
             "L1a": attention_fidelity_layer}
    with ExitStack() as ctx:
        x_sb = ctx.enter_context(nc.sbuf_tensor("x_sb", [P, NT, P], F32))
        const = load_constants(nc, ctx, x_sb, x, const_in)
        pool_dma = lambda n: ctx.enter_context(nc.semaphore(n))
        for name in ORDER:
            if name in steps:
                steps[name](nc, x_sb, const, layers[name], {"name": name + "_", "pool_dma": pool_dma})
            else:
                attention(nc, x_sb, const, layers[name], dict(ATTENTIONS[name], name=name + "_"))
        with nc.semaphore("stored") as stored, nc.Block() as block:

            @block.sync
            def _(sp):
                sp.dma_start(out.rearrange("b (t p) d -> p (b t) d", p=P), x_sb[:]).then_inc(stored, 16)
                sp.wait_ge(stored, 16)


ORDER = ["L0a", "L0x", "L0f", "L1a", "L1x", "L1f", "L2a", "L2x", "L2f", "L3a", "L3x", "L3f"]

def consts():
    i=np.arange(128)
    c={}
    c['ident']=np.eye(128,dtype=np.float32)
    c['ident_bf']=np.eye(128,dtype=np.float32)
    c['minus_half']=np.full((128,16),-0.5,np.float32)
    c['head_rows']=(i[:,None]//8==np.arange(16)[None]).astype(np.float32)
    mr=np.zeros((128,16,128),np.float32)
    for p in range(3):
        for h in range(16): mr[16*p+h,h]=1
    c['max_rows']=mr
    c['causal_q']=np.where(i[None,:]>i[:,None],np.float32(-1e30),np.float32(0))
    c['causal_k']=np.where(i[:,None]>i[None,:],np.float32(-1e30),np.float32(0))
    c['rank_down']=np.broadcast_to((32-np.arange(32)).astype(np.float32),(128,32)).copy()
    er=np.zeros((128,8,128),np.float32)
    for ch in range(8):
        for e in range(4): er[4*ch+e,ch,32*e:32*e+32]=1
    c['expert_rows']=er
    c['first_place']=np.broadcast_to((160*np.arange(16)).astype(np.float32),(128,16)).copy()
    c['before']=(i[:,None]<i[None,:]).astype(np.float32)
    c['first_token']=(256*(i//16)).astype(np.float32).reshape(128,1)
    c['rows_of_8']=((i[:,None]//8==np.arange(8)[None])).astype(np.float32)
    c['rows_of_16']=((i[:,None]//16==np.arange(8)[None])).astype(np.float32)
    pr=np.zeros((128,16,128),np.float32)
    for r in range(16): pr[r,r]=1
    c['pick_row']=pr
    c['ones_bf']=np.ones((128,128),np.float32)
    c['ones']=np.ones((128,128),np.float32)
    c['zero']=np.zeros((128,1),np.float32)
    return c
def rope_table():
    d=64
    inv=(1.0/10000.0**(np.arange(0,d,2,dtype=np.float32)/d)).astype(np.float32)
    f=np.outer(np.arange(256,dtype=np.float32),inv).astype(np.float32)
    f=np.concatenate([f,f],1)
    cos,sin=np.cos(f).T.astype(np.float32),np.sin(f).T.astype(np.float32)
    sgn=np.where(np.arange(64)<32,-1,1).astype(np.float32)[:,None]
    t=np.stack([cos,sin*sgn],1)
    return np.concatenate([t,t],0)
BF16_CONSTS=('ident_bf','max_rows','causal_q','causal_k','expert_rows','before','ones_bf')
A=np.ascontiguousarray
def col(a): return A(np.reshape(a,(-1,1)))
def row(a): return A(np.reshape(a,(1,-1)))
def rows_o(wo_in_out,H,hd):
    if hd==8:
        w=np.zeros((4,4,32,128),np.float32)
        w[:,:,0:8,:]=wo_in_out.reshape(4,4,8,128)
        return A(w.reshape(4,128,128).transpose(1,0,2))
    return A(wo_in_out.reshape(-1,128,128).transpose(1,0,2))
def layouts(I):
    D={}
    W={}
    W['w_q']=I['L0_attn_wq']; W['w_k']=I['L0_attn_wk_down']; W['w_v']=I['L0_attn_wv_down']
    ku=np.zeros((64,2,128),np.float32); ku[0:32,0]=I['L0_attn_wk_up']; ku[32:64,1]=I['L0_attn_wk_up']
    vu=np.zeros((64,2,128),np.float32); vu[0:32,0]=I['L0_attn_wv_up']; vu[32:64,1]=I['L0_attn_wv_up']
    W['k_up']=ku; W['v_up']=A(vu.reshape(64,256)); W['w_o']=rows_o(I['L0_attn_wo'],8,128)
    D['L0a']=W
    T=lambda a:A(np.asarray(a).T)
    dims=lambda a:A(np.asarray(a).reshape(a.shape[:-1]+(16,8)).swapaxes(-1,-2).reshape(a.shape))
    D['L0x']={'w_q':dims(T(I['L0_xattn_w_q'])),'w_k':dims(T(I['L0_xattn_w_k'])),'w_v':T(I['L0_xattn_w_v']),'w_o':rows_o(T(I['L0_xattn_w_o']),16,8)}
    for n,p in (('L1x','L1_xattn_'),('L3x','L3_xattn_')):
        D[n]={'w_q':dims(T(I[p+'Wq'])),'w_k':dims(T(I[p+'Wk'])),'w_v':T(I[p+'Wv']),'w_o':rows_o(T(I[p+'Wo']),16,8),
          'b_q':col(dims(I[p+'bq'])),'b_k':col(dims(I[p+'bk'])),'b_v':row(I[p+'bv']),'b_o':row(I[p+'bo'])}
    m=np.asarray(I['mask_SxS2_ik0'])
    D['L3x']['mask_q']=A(m.reshape(2,128,512).transpose(1,0,2).reshape(128,1024))
    D['L3x']['mask_k']=A(m.T.reshape(4,128,256).transpose(1,0,2).reshape(128,1024))
    wq=np.asarray(I['L2_attn_Wq']).reshape(128,16,64)
    pairs=L2_PAIRS
    order=[h for p in pairs for h in p]
    half=lambda a: np.concatenate([a[...,32:],a[...,:32]],-1)
    wqc=wq[:,order]
    wkv=np.asarray(I['L2_attn_Wkv']).reshape(128,8,64)
    D['L2a']={'w_q':A(wqc.reshape(128,1024)),'w_qr':A(half(wqc).reshape(128,1024)),'w_k':A(wkv[:,:4].reshape(128,256)),
      'w_kr':A(half(wkv[:,:4]).reshape(128,256)),'w_v':A(wkv[:,4:].reshape(128,256)),'w_o':rows_o(np.asarray(I['L2_attn_Wo']),16,64),
      'b_o':row(I['L2_attn_bo']),'cos_sin':rope_table()}
    wa=np.asarray(I['L3_attn_Wa']).reshape(16,3,64,128)
    f=lambda k:A(wa[:,k].reshape(1024,128).T)
    D['L3a']={'w_q':f(0),'w_k':f(1),'w_v':f(2),'w_o':rows_o(T(I['L3_attn_Wout_w']),16,64),'b_o':row(I['L3_attn_Wout_b'])}
    m=np.asarray(I['mask_BxSxS2_ik1'])
    mq=m.reshape(8,2,128,512).transpose(0,2,1,3).reshape(8,128,1024)
    mk=m.transpose(0,2,1).reshape(8,4,128,256).transpose(0,2,1,3).reshape(8,128,1024)
    p='L2_xattn_'
    D['L2x']={'w_q':np.asarray(I[p+'Wq']),'w_k':np.asarray(I[p+'Wk']),'w_v':np.asarray(I[p+'Wv']),'w_o':np.eye(128,dtype=np.float32).reshape(128,1,128),
          'b_q':col(I[p+'bq']),'b_k':col(I[p+'bk']),'b_v':row(I[p+'bv']),'masks':A(np.stack([mq,mk],2))}
    p='L3_ffn_'
    b2=np.zeros((128,128),np.float32); b2[:32]=I[p+'bias2']
    D['L3f']={'w_r':T(I[p+'router_w']),'b_r':row(I[p+'router_b']),'w_1':A(np.asarray(I[p+'weights1']).transpose(1,0,2).reshape(128,1024)),
      'b_1':A(np.asarray(I[p+'bias1']).reshape(8,128).T),'w_2':A(np.asarray(I[p+'weights2']).reshape(8,128,128).transpose(1,0,2)),'b_2':b2}
    p='L2_ffn_'
    cat=lambda a,b: np.concatenate([np.asarray(I[p+a]),np.asarray(I[p+b])[None]],0)
    g,u_,d_=cat('expert_gate','shared_gate'),cat('expert_up','shared_up'),cat('expert_down','shared_down')
    wd=np.zeros((128,9,3,128),np.float32)
    dt=d_.transpose(0,2,1)
    for i,(c0,n) in enumerate([(0,128),(128,128),(256,96)]): wd[:n,:,i]=dt[:,c0:c0+n].transpose(1,0,2)
    D['L2f']={'w_r':T(I[p+'gate_w']),'w_g':A(g.transpose(2,0,1)),'w_u':A(u_.transpose(2,0,1)),'w_d':wd}
    p='L0_ffn_'
    D['L0f']={'w_r':T(I[p+'gate_w']),'w_1':np.asarray(I[p+'w1']),'w_2':A(np.asarray(I[p+'w2']).reshape(16,4,128,128).transpose(0,2,1,3))}
    p='L1_ffn_'
    D['L1f']={'w_r':T(I[p+'gate_query']),'log_temp':np.asarray(I[p+'log_temp']).reshape(1,1),'w_1':np.asarray(I[p+'w1']),'w_2':A(np.asarray(I[p+'w2']).reshape(16,4,128,128).transpose(0,2,1,3)),
      'b_1':A(np.asarray(I[p+'b1']).reshape(16,4,128).transpose(0,2,1)),'b_2':np.asarray(I[p+'b2'])}
    p='L1_attn_'
    hh=lambda a:A(np.asarray(a).transpose(1,0,2).reshape(128,128))
    wc=np.zeros((8,16,8,8),np.float32)
    for k in range(8): wc[k,:,k,:]=np.asarray(I[p+'Wc2q'])[k]
    wo=np.zeros((2,4,32,128),np.float32); wo[:,:,0:16]=np.asarray(I[p+'Wo']).reshape(2,4,16,128)
    D['L1a']={'w_q':hh(I[p+'Wq']),'w_k':hh(I[p+'Wk']),'w_v':hh(I[p+'Wv']),'b_q':col(I[p+'bq']),'b_k':col(I[p+'bk']),'b_v':row(I[p+'bv']),
      'w_c':A(wc.reshape(128,64)),'b_c':col(I[p+'bc2q']),'b_cr':row(I[p+'bc2q']),'w_o':A(wo.reshape(2,128,128).transpose(1,0,2)),'b_o':row(I[p+'bo']),
      'g1c':col(I[p+'g1']),'beta1c':col(I[p+'beta1']),'rows':A(np.stack([I[p+'g1'],I[p+'beta1'],I[p+'g2'],I[p+'beta2']])),
      'w_1':np.asarray(I[p+'W1']),'b_1':A(np.asarray(I[p+'b1']).reshape(4,128).T),'w_m':A(np.asarray(I[p+'Wm']).reshape(4,128,8).transpose(1,0,2)),
      'b_m':col(I[p+'bm']),'w_qo':np.asarray(I[p+'Wqo']),'b_qo':A(np.asarray(I[p+'bqo']).reshape(4,128).T),
      'w_2':A(np.asarray(I[p+'W2']).reshape(4,128,128).transpose(1,0,2)),'b_2':col(I[p+'b2'])}
    ctxT=A(np.asarray(I['ctx_1024']).transpose(0,2,1))
    D['ctxT']=ctxT
    return D
L2_PAIRS=[(a,a+4) for a in range(4)]+[(8+a,12+a) for a in range(4)]
ATTENTIONS={
 'L0a':dict(heads=8,hd=128,nkeys=256,causal=True,kchunks=2,vcols=256,latent=True,scale=128**-0.5,kchunk=lambda h:h//4,vhead=lambda h:h//4),
 'L0x':dict(heads=16,hd=8,nkeys=512,cross=True,kchunks=1,vcols=128,scale=8**-0.5,kchunk=lambda h:0),
 'L1x':dict(heads=16,hd=8,nkeys=512,cross=True,kchunks=1,vcols=128,scale=8**-0.5,kchunk=lambda h:0,qk_bias=True,out_bias=True),
 'L3x':dict(heads=16,hd=8,nkeys=512,cross=True,kchunks=1,vcols=128,scale=8**-0.5,kchunk=lambda h:0,qk_bias=True,out_bias=True,masked=True),
 'L2x':dict(heads=1,hd=128,nkeys=512,cross=True,kchunks=1,vcols=128,scale=128**-0.5,kchunk=lambda h:0,vhead=lambda h:0,qk_bias=True,mask_each=True),
 'L2a':dict(heads=16,hd=64,nkeys=256,kchunks=2,vcols=256,rope=True,scale=64**-0.5,kchunk=lambda h:h//8,vhead=lambda h:h//4,out_bias=True,pairs=L2_PAIRS),
 'L3a':dict(heads=16,hd=64,nkeys=256,causal=True,kchunks=8,vcols=1024,scale=64**-0.5,kchunk=lambda h:h//2,vhead=lambda h:h,out_bias=True,pairs=[(2*a,2*a+1) for a in range(8)]),
}


def kernel(**inputs):
    import concourse.bacc as bacc
    from concourse.bass_utils import run_bass_kernel_spmd

    nc = bacc.Bacc("TRN2", target_bir_lowering=False, num_devices=1)
    arrays = {}

    def dram(name, a):
        arrays[name] = np.ascontiguousarray(a)
        return nc.dram_tensor(name, arrays[name].shape, mybir.dt.from_np(arrays[name].dtype), kind="ExternalInput").ap()

    inputs = {n: np.asarray(a) for n, a in inputs.items()}
    x = dram("x", inputs["x"])
    const_in = {n: dram("const_in_" + n, a) for n, a in consts().items()}
    laid = layouts(inputs)
    ctxT = dram("ctxT", laid.pop("ctxT"))
    layers = {name: {n: dram(name + "_in_" + n, a) for n, a in laid[name].items()} for name in ORDER}
    for name in ORDER:
        layers[name]["ctxT"] = ctxT
    out = nc.dram_tensor("out", (B, S, P), F32, kind="ExternalOutput").ap()
    decoder(nc, x, out, const_in, layers)
    got = run_bass_kernel_spmd(nc, [arrays], core_ids=[0])
    return got.results[0]["out"]
```
